# Optimizing a Trainium2 kernel written in Bass

```python
import numpy as np
import jax
import jax.numpy as jnp

def _softmax(x, axis=-1):
    return jax.nn.softmax(x, axis=axis)

def _gelu(x):
    return jax.nn.gelu(x, approximate=True)

def _silu(x):
    return jax.nn.silu(x)

def _sigmoid(x):
    return jax.nn.sigmoid(x)

def _layernorm(x, axis=-1, eps=1e-05):
    m = jnp.mean(x, axis=axis, keepdims=True)
    v = jnp.var(x, axis=axis, keepdims=True)
    return (x - m) / jnp.sqrt(v + eps)

def _scatter_add(tgt, idx, src, axis=0):
    return tgt.at[idx].add(src)

def _segment_sum(src, seg, n):
    return jax.ops.segment_sum(src, seg, n)
kernel_name = 'mk_adj_preln_d4_adj_r2_8a1602'

def setup_inputs(seed: int=0):
    np.random.seed(seed)
    _w = jnp.asarray

    def _rec_inputs():
        import jax
        import jax.numpy as jnp
        _gk = jax.random.key(seed)
        x = 7.22e-05 + 1 * jax.random.normal(jax.random.fold_in(_gk, 1), (64, 128, 256), jnp.float32)
        _a = jax.random.bernoulli(jax.random.fold_in(_gk, 2), 0.0625, (128, 128))
        _af = _a.astype(jnp.float32)
        adj = _af
        return (x, adj)
    x, adj = _rec_inputs()

    def _L0_gnn_setup():
        import jax, jax.numpy as jnp
        import numpy as np
        B, N, D = (8, 1024, 256)
        key = jax.random.key(seed)
        k1, k2, k3, k4, k5 = jax.random.split(key, 5)
        neuron_states = jax.random.normal(k1, (B, N, D), dtype=jnp.float32)
        adjacency = jax.random.randint(k2, (N, N), 0, 2).astype(jnp.float32)
        scale = 1.0 / np.sqrt(D)
        Wq = jax.random.normal(k3, (D, D), dtype=jnp.float32) * scale
        Wk = jax.random.normal(k4, (D, D), dtype=jnp.float32) * scale
        Wv = jax.random.normal(k5, (D, D), dtype=jnp.float32) * scale
        return {'neuron_states': neuron_states, 'adjacency': adjacency, 'Wq': Wq, 'Wk': Wk, 'Wv': Wv}
    _L0_gnn_all = _L0_gnn_setup()
    _L0_gnn_in = {k: v for k, v in _L0_gnn_all.items() if k in ('Wq', 'Wk', 'Wv')}
    del _L0_gnn_all

    def _L1_gnn_setup():
        import jax, jax.numpy as jnp
        import numpy as np
        B, N, D, H = (4, 1024, 256, 8)
        HD = D // H
        key = jax.random.key(seed)
        ks = jax.random.split(key, 10)
        x = jax.random.normal(ks[0], (B, N, D), dtype=jnp.float32)
        adj = (jax.random.uniform(ks[1], (N, N)) < 0.1).astype(jnp.float32)
        s = 1.0 / np.sqrt(D)
        Wq = jax.random.normal(ks[2], (D, D), dtype=jnp.float32) * s
        Wk = jax.random.normal(ks[3], (D, D), dtype=jnp.float32) * s
        Wv = jax.random.normal(ks[4], (D, D), dtype=jnp.float32) * s
        Wo = jax.random.normal(ks[5], (D, D), dtype=jnp.float32) * s
        bq = jnp.zeros((D,), jnp.float32)
        bk = jnp.zeros((D,), jnp.float32)
        bv = jnp.zeros((D,), jnp.float32)
        bo = jnp.zeros((D,), jnp.float32)
        return {'x': x, 'adj': adj, 'Wq': Wq, 'bq': bq, 'Wk': Wk, 'bk': bk, 'Wv': Wv, 'bv': bv, 'Wo': Wo, 'bo': bo}
    _L1_gnn_all = _L1_gnn_setup()
    _L1_gnn_in = {k: v for k, v in _L1_gnn_all.items() if k in ('Wq', 'bq', 'Wk', 'bk', 'Wv', 'bv', 'Wo', 'bo')}
    del _L1_gnn_all

    def _L2_gnn_setup():
        import jax, jax.numpy as jnp
        import numpy as np
        ALPHA = 0.2
        key = jax.random.key(seed)
        k0, k1, k2, k3 = jax.random.split(key, 4)
        B, N, C, F = (64, 512, 256, 256)
        x = jax.random.normal(k0, (B, N, C), dtype=jnp.float32)
        W = jax.random.normal(k1, (C, F), dtype=jnp.float32) * (1.414 / np.sqrt(C + F))
        a = jax.random.normal(k2, (2 * F, 1), dtype=jnp.float32) * (1.414 / np.sqrt(2 * F + 1))
        beta = jnp.ones((1,), dtype=jnp.float32)
        mask = (jax.random.uniform(k3, (N, N)) < 0.3).astype(jnp.float32)
        return {'x': x, 'W': W, 'a': a, 'beta': beta, 'mask': mask}
    _L2_gnn_all = _L2_gnn_setup()
    _L2_gnn_in = {k: v for k, v in _L2_gnn_all.items() if k in ('W', 'a', 'beta')}
    del _L2_gnn_all

    def _L3_gnn_setup():
        import jax, jax.numpy as jnp
        import numpy as np
        B, N, F_IN, F_OUT = (16, 1024, 256, 256)
        key = jax.random.key(seed)
        k1, k2, k3 = jax.random.split(key, 3)
        x = jax.random.normal(k1, (B, N, F_IN), dtype=jnp.float32)
        adj = jax.random.uniform(k2, (N, N), dtype=jnp.float32)
        bound = np.sqrt(6.0 / F_OUT)
        weight = jax.random.uniform(k3, (F_IN, F_OUT), dtype=jnp.float32, minval=-bound, maxval=bound)
        bias = jnp.zeros((F_OUT,), dtype=jnp.float32)
        return {'x': x, 'adj': adj, 'weight': weight, 'bias': bias}
    _L3_gnn_all = _L3_gnn_setup()
    _L3_gnn_in = {k: v for k, v in _L3_gnn_all.items() if k in ('weight', 'bias')}
    del _L3_gnn_all
    return {'x': x, 'adj': adj, 'L0_gnn_Wq': _L0_gnn_in['Wq'], 'L0_gnn_Wk': _L0_gnn_in['Wk'], 'L0_gnn_Wv': _L0_gnn_in['Wv'], 'L1_gnn_Wq': _L1_gnn_in['Wq'], 'L1_gnn_bq': _L1_gnn_in['bq'], 'L1_gnn_Wk': _L1_gnn_in['Wk'], 'L1_gnn_bk': _L1_gnn_in['bk'], 'L1_gnn_Wv': _L1_gnn_in['Wv'], 'L1_gnn_bv': _L1_gnn_in['bv'], 'L1_gnn_Wo': _L1_gnn_in['Wo'], 'L1_gnn_bo': _L1_gnn_in['bo'], 'L2_gnn_W': _L2_gnn_in['W'], 'L2_gnn_a': _L2_gnn_in['a'], 'L2_gnn_beta': _L2_gnn_in['beta'], 'L3_gnn_weight': _L3_gnn_in['weight'], 'L3_gnn_bias': _L3_gnn_in['bias']}

def reference(x, adj, L0_gnn_Wq, L0_gnn_Wk, L0_gnn_Wv, L1_gnn_Wq, L1_gnn_bq, L1_gnn_Wk, L1_gnn_bk, L1_gnn_Wv, L1_gnn_bv, L1_gnn_Wo, L1_gnn_bo, L2_gnn_W, L2_gnn_a, L2_gnn_beta, L3_gnn_weight, L3_gnn_bias):
    import jax
    import jax.numpy as jnp

    def _L0_gnn_ref(neuron_states, adjacency, Wq, Wk, Wv):
        import jax, jax.numpy as jnp
        import numpy as np
        B, N, D = (8, 1024, 256)
        q = jnp.einsum('bnd,ed->bne', neuron_states, Wq)
        k = jnp.einsum('bnd,ed->bne', neuron_states, Wk)
        v = jnp.einsum('bnd,ed->bne', neuron_states, Wv)
        rel = jnp.einsum('bnd,bmd->bnm', q, k)
        rel = adjacency.T[None, :, :] * rel
        rel = rel / jnp.linalg.norm(rel, axis=2, keepdims=True)
        return jnp.einsum('bnm,bmd->bnd', rel, v)

    def _L1_gnn_ref(x, adj, Wq, bq, Wk, bk, Wv, bv, Wo, bo):
        import jax, jax.numpy as jnp
        import numpy as np
        B, N, D, H = (4, 1024, 256, 8)
        HD = D // H
        b, n, d = x.shape
        q = (x @ Wq + bq).reshape(b, n, H, HD)
        k = (x @ Wk + bk).reshape(b, n, H, HD)
        v = (x @ Wv + bv).reshape(b, n, H, HD)
        scores = jnp.einsum('bqhd,bkhd->bhqk', q, k) / jnp.sqrt(jnp.float32(HD))
        scores = scores + (1.0 - adj)[None, None, :, :] * -1000000000.0
        attn = jax.nn.softmax(scores, axis=-1)
        out = jnp.einsum('bhqk,bkhd->bqhd', attn, v).reshape(b, n, d)
        return out @ Wo + bo

    def _L2_gnn_ref(x, W, a, beta, mask):
        import jax, jax.numpy as jnp
        import numpy as np
        ALPHA = 0.2
        F_ = W.shape[1]
        h = jnp.einsum('bnc,cf->bnf', x, W)
        a1, a2 = (a[:F_, 0], a[F_:, 0])
        s1 = jnp.einsum('bnf,f->bn', h, a1)
        s2 = jnp.einsum('bnf,f->bn', h, a2)
        e = jax.nn.leaky_relu(s1[:, :, None] + s2[:, None, :], negative_slope=ALPHA)
        e = e * mask[None, :, :]
        att = jax.nn.softmax(e, axis=2)
        h_prime = jnp.einsum('bij,bjf->bif', att, h)
        return jax.nn.elu(h_prime + beta * h)

    def _L3_gnn_ref(x, adj, weight, bias):
        import jax, jax.numpy as jnp
        import numpy as np
        B, N, F_IN, F_OUT = (16, 1024, 256, 256)
        deg = adj.sum(axis=1)
        deg_inv_sqrt = jnp.where(deg > 0, jax.lax.rsqrt(deg), 0.0)
        norm_adj = adj * deg_inv_sqrt[:, None] * deg_inv_sqrt[None, :]
        support = jnp.einsum('bni,io->bno', x, weight)
        output = jnp.einsum('nm,bmo->bno', norm_adj, support)
        return output + bias
    h = jnp.maximum(_layernorm(x, axis=-1), 0.0)
    x = x + _L0_gnn_ref(h, adj, L0_gnn_Wq, L0_gnn_Wk, L0_gnn_Wv)
    h = jnp.maximum(_layernorm(x, axis=-1), 0.0)
    x = x + _L1_gnn_ref(h, adj, L1_gnn_Wq, L1_gnn_bq, L1_gnn_Wk, L1_gnn_bk, L1_gnn_Wv, L1_gnn_bv, L1_gnn_Wo, L1_gnn_bo)
    h = jnp.maximum(_layernorm(x, axis=-1), 0.0)
    x = x + _L2_gnn_ref(h, L2_gnn_W, L2_gnn_a, L2_gnn_beta, adj)
    h = jnp.maximum(_layernorm(x, axis=-1), 0.0)
    x = x + _L3_gnn_ref(h, adj, L3_gnn_weight, L3_gnn_bias)
    return x

_drawn_inputs = setup_inputs


def setup_inputs(seed=0):
    import zlib

    import numpy as np

    out = dict(_drawn_inputs(seed))
    spreads = {'L1_gnn_bq': (0.0, 0.8),
     'L1_gnn_bk': (0.0, 0.8),
     'L1_gnn_bv': (0.0, 0.1),
     'L1_gnn_bo': (0.0, 0.1),
     'L3_gnn_bias': (0.0, 0.1)}
    factors = {'L2_gnn_a': 8.0}
    for name, (base, spread) in spreads.items():
        noise = np.random.default_rng([zlib.crc32(name.encode()), seed]).standard_normal(out[name].shape)
        drawn = base * np.exp(spread * noise) if base else spread * noise
        out[name] = jnp.asarray(drawn.astype(out[name].dtype))
    for name, factor in factors.items():
        out[name] = (out[name] * factor).astype(out[name].dtype)
    return out
```

```python
from contextlib import ExitStack

import concourse.bass as bass
from concourse import mybir

ALU = mybir.AluOpType
ACT = mybir.ActivationFunctionType
F32 = mybir.dt.float32
F32R = mybir.dt.float32r
AX_X = mybir.AxisListType.X


def four_layer_graph_kernel(nc, x, adj, L0_gnn_Wq, L0_gnn_Wk, L0_gnn_Wv,
                            L1_gnn_Wq, L1_gnn_bq, L1_gnn_Wk, L1_gnn_bk, L1_gnn_Wv, L1_gnn_bv,
                            L1_gnn_Wo, L1_gnn_bo, L2_gnn_W, L2_gnn_a, L2_gnn_beta,
                            L3_gnn_weight, L3_gnn_bias, out):
    B, N, D = x.shape
    P = 128
    GB = 4
    G = B // GB
    C = D // P
    GN = GB * N
    GD = GB * D
    H = 8
    HD = D // H
    R = P // HD
    PB = 2
    NP = B // PB
    EPS = 1e-05
    ALPHA = 0.2
    BIG = 1000000000.0
    TINY = 1e-30
    assert N == P and GN == 512 and C == 2 and R == 4

    ctx = ExitStack()
    with ctx:
        def sb(name, shape, dt=F32):
            return ctx.enter_context(nc.sbuf_tensor(name, shape, dt))

        def sem(name):
            return ctx.enter_context(nc.semaphore(name))

        ps = ctx.enter_context(nc.psum_tensor("ps", [P, 8, 512], F32))

        xs = sb("xs", [P, B * D])
        adj_n = sb("adj_n", [P, N])
        ident = sb("ident", [P, P])
        ones = sb("ones", [P, P])
        maskb = sb("maskb", [P, N])
        beta_i = sb("beta_i", [P, N])
        beta_c = sb("beta_c", [P, 1])
        deg = sb("deg", [P, 1])
        deg_pos = sb("deg_pos", [P, 1])
        deg_safe = sb("deg_safe", [P, 1])
        deg_pow = sb("deg_pow", [P, 1])
        dis = sb("dis", [P, 1])
        adj_s = sb("adj_s", [P, N])
        norm_adj_t = sb("norm_adj_t", [P, N])
        expo = sb("expo", [P, 8])
        eps_c = sb("eps_c", [P, GB])
        bo_row = sb("bo_row", [P, D])
        b3_row = sb("b3_row", [P, D])
        bq_c = sb("bq_c", [P, C])
        bqs_c = sb("bqs_c", [P, C])
        bk_c = sb("bk_c", [P, C])
        bv_c = sb("bv_c", [P, C])
        bv_rep = sb("bv_rep", [P, C, P])
        a_row = sb("a_row", [P, 2, D])
        wq0 = sb("wq0", [P, C, D])
        wk0 = sb("wk0", [P, C, D])
        wv0 = sb("wv0", [P, C, D])
        wstage = sb("wstage", [P, 4, C, D])
        w_o = sb("w_o", [P, C, D])
        w2x = sb("w2x", [P, C, D + 2])
        w2c = sb("w2c", [P, C, 2])
        w2junk = sb("w2junk", [P, D])
        w2rep = sb("w2rep", [P, C, P])
        m_hi, m_lo = sb("m_hi", [P, C, D], F32R), sb("m_lo", [P, C, D], F32R)
        v0_hi, v0_lo = sb("v0_hi", [P, C, D], F32R), sb("v0_lo", [P, C, D], F32R)
        q1_hi, q1_lo = sb("q1_hi", [P, C, D], F32R), sb("q1_lo", [P, C, D], F32R)
        k1_hi, k1_lo = sb("k1_hi", [P, C, D], F32R), sb("k1_lo", [P, C, D], F32R)
        v1_hi, v1_lo = sb("v1_hi", [P, C, D], F32R), sb("v1_lo", [P, C, D], F32R)
        w3_hi, w3_lo = sb("w3_hi", [P, C, D], F32R), sb("w3_lo", [P, C, D], F32R)
        w2_hi, w2_lo = sb("w2_hi", [P, C, D + 2], F32R), sb("w2_lo", [P, C, D + 2], F32R)
        s2_hi, s2_lo = sb("s2_hi", [P, C, P], F32R), sb("s2_lo", [P, C, P], F32R)
        st = sb("st", [P, GB, 6])
        st_seen = sb("st_seen", [P, 1])
        mv = sb("mv", [P, GB, 2])
        veps = sb("veps", [P, GB])
        rstd = sb("rstd", [P, GB])
        nmr = sb("nmr", [P, GB])
        xn = sb("xn", [P, GB, D])
        h_t = sb("h_t", [P, C, GN])
        h_hi = sb("h_hi", [P, C, GN], F32R)
        h_lo = sb("h_lo", [P, C, GN], F32R)
        buf_a = sb("buf_a", [P, C, GN])
        buf_b = sb("buf_b", [P, C, GN])
        vals = sb("vals", [P, 2, GB, D])
        rel = sb("rel", [P, GN])
        rel2 = sb("rel2", [P, GN])
        nrm = sb("nrm", [P, GB])
        rnrm = sb("rnrm", [P, GB])
        sc = sb("sc", [P, PB, R, C, N])
        mx = sb("mx", [P, PB, R * C])
        pr = sb("pr", [P, 2, PB, R, C, N])
        sums = sb("sums", [P, PB, C, R])
        rinv = sb("rinv", [P, PB, C, R])
        rinv_x = sb("rinv_x", [P, PB, C, P])
        rinv_t = sb("rinv_t", [P, C, PB * N])
        pr_t = sb("pr_t", [P, 2, R, N])
        o_t = sb("o_t", [P, C, PB * N])
        s1 = sb("s1", [P, GB])
        e2 = sb("e2", [P, GB, N])
        p2 = sb("p2", [P, GB, N])
        p2_t = sb("p2_t", [P, GB, N])
        mx2 = sb("mx2", [P, GB])
        sum2 = sb("sum2", [P, GB])
        ri2 = sb("ri2", [P, GB])
        a_hi = sb("a_hi", [P, 2, C, GN], F32R)
        a_lo = (h_hi, h_lo)

        sems = {}

        def S(name):
            if name not in sems:
                sems[name] = sem(name)
            return sems[name]

        w_in, x_in, x_out = S("w_in"), S("x_in"), S("x_out")
        su_pool, su_dve, su_pe, su_act = S("su_pool"), S("su_dve"), S("su_pe"), S("su_act")
        bn_done, stat_ready, veps_done, rstd_ready, nmr_ready = S("bn_done"), S("stat_ready"), S("veps_done"), S("rstd_ready"), S("nmr_ready")
        xn_ready, turned, ht_ready, hi_ready, lo_ready = S("xn_ready"), S("turned"), S("ht_ready"), S("hi_ready"), S("lo_ready")

        def xg(g, b=0, nb=GB):
            return xs[:, bass.ds(g * GD + b * D, nb * D)]

        def bc(ap, reps):
            return ap.unsqueeze(1).broadcast_to([P, reps, N])

        def bcol(ap, cols):
            return ap.unsqueeze(2).broadcast_to([P, ap.shape[1], cols])

        def f32(ap):
            return ap.bitcast(F32)

        weights = [L1_gnn_Wq, L1_gnn_Wk, L1_gnn_Wv, L3_gnn_weight]
        loads = [(adj_n[:], adj)]
        loads += [(t[:], w.rearrange("(c p) f -> p c f", p=P))
                  for t, w in ((wq0, L0_gnn_Wq), (wk0, L0_gnn_Wk), (wv0, L0_gnn_Wv), (w_o, L1_gnn_Wo))]
        loads += [(wstage[:, i], w.rearrange("(c p) f -> p c f", p=P)) for i, w in enumerate(weights)]
        loads += [(w2x[:, :, 0:D], L2_gnn_W.rearrange("(c p) f -> p c f", p=P))]
        loads += [(a_row[:], L2_gnn_a.rearrange("(t f) o -> (o t) f", t=2).partition_broadcast(P))]
        loads += [(t[:], v.partition_broadcast(P)) for t, v in
                  ((bo_row, L1_gnn_bo), (b3_row, L3_gnn_bias), (beta_c, L2_gnn_beta))]
        loads += [(t[:], v.rearrange("(c p) -> p c", p=P)) for t, v in
                  ((bq_c, L1_gnn_bq), (bk_c, L1_gnn_bk), (bv_c, L1_gnn_bv))]
        NLOAD = len(loads)

        block = ctx.enter_context(nc.Block())

        @block.sync
        def _(sp):
            with nc.allow_non_contiguous_dma(reason="bias columns"):
                for dst, src in loads[:4]:
                    sp.dma_start(dst, src).then_inc(w_in, 16)
                for g in range(2):
                    sp.dma_start(xg(g).rearrange("p (b d) -> p b d", b=GB),
                                 x[g * GB:(g + 1) * GB].rearrange("b n d -> n b d")).then_inc(x_in, 16)
                    sp.wait_ge(x_in, 16 * (g + 1))
                for dst, src in loads[4:]:
                    sp.dma_start(dst, src).then_inc(w_in, 16)
            with sp.Fori(2, G) as g:
                sp.wait_ge(x_in, g * 16)
                sp.dma_start(xg(g).rearrange("p (b d) -> p b d", b=GB),
                             x[bass.ds(g * GB, GB)].rearrange("b n d -> n b d")).then_inc(x_in, 16)
            with sp.Fori(0, G) as g:
                sp.wait_ge(S("fin3"), g + 1)
                sp.dma_start(out[bass.ds(g * GB, GB)].rearrange("b n d -> n b d"),
                             xg(g).rearrange("p (b d) -> p b d", b=GB)).then_inc(x_out, 16)
            sp.wait_ge(x_out, 16 * G)

        @block.tensor
        def _(pe):
            def split3(o, lhs, rhs, which, first=True, last=True):
                terms = {"hi": [(0, 0), (0, 1)], "lo": [(1, 0)], "all": [(0, 0), (0, 1), (1, 0)]}[which]
                steps = [(a, b, c) for a, b in terms for c in range(C)]
                for i, (a, b, c) in enumerate(steps):
                    m = pe.matmul(o, lhs[a](c), rhs[b](c), start=first and i == 0,
                                  stop=last and i == len(steps) - 1, skip_group_check=True)
                return m

            def proj_t(bank, w_hi, w_lo, which):
                for f in range(C):
                    for a, hb in (("hi", h_hi), ("lo", h_lo)):
                        if a != which:
                            continue
                        ws = (w_hi, w_lo) if a == "hi" else (w_hi,)
                        for wi, w in enumerate(ws):
                            for c in range(C):
                                m = pe.matmul(ps[:, bank + f, :], w[:, c, f * P:(f + 1) * P], hb[:, c, :],
                                              start=(a == "hi" and wi == 0 and c == 0),
                                              stop=(a == "lo" and c == C - 1), skip_group_check=True)
                return m

            def proj_n(o, b, w_hi, w_lo):
                cols = slice(b * N, (b + 1) * N)
                return split3(o, (lambda c: h_hi[:, c, cols], lambda c: h_lo[:, c, cols]),
                              (lambda c: w_hi[:, c, :], lambda c: w_lo[:, c, :]), "all")

            def turn(n, bank):
                pe.wait_ge(xn_ready, n + 1)
                for c in range(C):
                    for b in range(GB):
                        m = pe.transpose(ps[:, bank + c, b * N:(b + 1) * N], xn[:, b, c * P:(c + 1) * P], ident[:])
                m.then_inc(turned, 1)

            pe.wait_ge(w_in, 16 * NLOAD)
            pe.wait_ge(su_pool, 1)
            for dc in range(C):
                for ec in range(C):
                    m = pe.matmul(ps[:, dc, 0:D], wq0[:, ec, dc * P:(dc + 1) * P], wk0[:, ec, :],
                                  start=(ec == 0), stop=(ec == C - 1))
            for dc in range(C):
                for ec in range(C):
                    m = pe.transpose(ps[:, 2 + dc, ec * P:(ec + 1) * P], wv0[:, ec, dc * P:(dc + 1) * P], ident[:])
            m.then_inc(su_pe, 1)
            pe.wait_ge(su_dve, 1)
            pe.transpose(ps[:, 4, 0:N], adj_s[:], ident[:])
            for c in range(C):
                m = pe.matmul(ps[:, 7, 0:D], bv_rep[:, c, :], w_o[:, c, :], start=(c == 0), stop=(c == C - 1))
            m.then_inc(su_pe, 1)
            turn(0, 5)
            pe.wait_ge(su_dve, 2)

            def l0(g, first):
                pe.wait_ge(hi_ready, g + 1)
                proj_t(0, m_hi, m_lo, "hi")
                pe.wait_ge(lo_ready, g + 1)
                proj_t(0, m_hi, m_lo, "lo").then_inc(S("g_done"), 1)
                if not first:
                    pe.wait_ge(S("fin0"), g)
                for b in range(GB):
                    m = proj_n(ps[:, 2 + b // 2, (b % 2) * D:(b % 2 + 1) * D], b, v0_hi, v0_lo)
                m.then_inc(S("v_done"), 1)
                pe.wait_ge(S("gt_ready"), g + 1)
                for b in range(GB):
                    for c in range(C):
                        m = pe.matmul(ps[:, 4, b * N:(b + 1) * N], h_t[:, c, b * N:(b + 1) * N],
                                      buf_a[:, c, b * N:(b + 1) * N], start=(c == 0), stop=(c == C - 1))
                m.then_inc(S("rel_done"), 1)
                turn(g + 1, 5)
                pe.wait_ge(S("rel_ready"), g + 1)
                pe.wait_ge(S("v_ready"), g + 1)
                for b in range(GB):
                    m = pe.matmul(ps[:, 2 + b // 2, (b % 2) * D:(b % 2 + 1) * D], rel[:, b * N:(b + 1) * N],
                                  vals[:, 0, b, :], start=True, stop=True)
                m.then_inc(S("out0_done"), 1)
                pe.wait_ge(S("rel2_ready"), g + 1)
                for b in range(GB):
                    m = pe.matmul(ps[:, 7, b:b + 1], rel2[:, b * N:(b + 1) * N], ones[:, 0:1], start=True, stop=True)
                m.then_inc(S("nrm_done"), 1)

            l0(0, True)
            with pe.Fori(1, G - 1) as g:
                l0(g, False)
            l0(G - 1, False)

            def qk(g, first):
                pe.wait_ge(hi_ready, g + G + 1)
                proj_t(4, q1_hi, q1_lo, "hi")
                if not first:
                    pe.wait_ge(S("fin1"), 2 * g - 1)
                proj_t(6, k1_hi, k1_lo, "hi")
                pe.wait_ge(lo_ready, g + G + 1)
                proj_t(4, q1_hi, q1_lo, "lo").then_inc(S("q_done"), 1)
                proj_t(6, k1_hi, k1_lo, "lo").then_inc(S("k_done"), 1)

            def scores(g, half):
                p = 2 * g + half
                for b2 in range(PB):
                    cols = slice((2 * half + b2) * N, (2 * half + b2 + 1) * N)
                    for f in range(C):
                        for r in range(R):
                            rows = slice(r * HD, (r + 1) * HD)
                            o = b2 * C * N + f * N
                            m = pe.matmul(ps[:, r, o:o + N], buf_a[rows, f, cols], buf_b[rows, f, cols],
                                          start=True, stop=True)
                m.then_inc(S("s_done"), 1)

            def scores_wait(g, half):
                pe.wait_ge(S("q_ready"), g + 1)
                pe.wait_ge(S("k_ready"), g + 1)
                pe.wait_ge(S("masked"), 4 * g + 2 * half)

            def attend(g, half, p):
                def turn_p(j):
                    b2, f = divmod(j, C)
                    if j >= 2:
                        pe.wait_ge(S("pt_ready"), 4 * p + j - 1)
                    for r in range(R):
                        m = pe.transpose(ps[:, 4 + f, r * N:(r + 1) * N], pr[:, half, b2, r, f, :], ident[:])
                    m.then_inc(S("pt_done"), 1)

                def apply_p(j):
                    b2, f = divmod(j, C)
                    pe.wait_ge(S("pt_ready"), 4 * p + j + 1)
                    o = f * PB * N + b2 * N
                    for r in range(R):
                        v_cols = slice(f * P + r * HD, f * P + (r + 1) * HD)
                        m = pe.matmul(ps[r * HD:(r + 1) * HD, 6, o:o + N], vals[:, 0, 2 * half + b2, v_cols],
                                      pr_t[:, j % 2, r, :], start=True, stop=True)
                    return m

                pe.wait_ge(S("fin1"), p)
                pe.wait_ge(S("spread"), p + 1)
                for b2 in range(PB):
                    for f in range(C):
                        o = f * PB * N + b2 * N
                        m = pe.transpose(ps[:, 7, o:o + N], rinv_x[:, b2, f, :], ident[:])
                m.then_inc(S("rt_done"), 1)
                turn_p(0)
                turn_p(1)
                apply_p(0)
                turn_p(2)
                apply_p(1)
                turn_p(3)
                apply_p(2)
                apply_p(3).then_inc(S("pv_done"), 1)
                pe.wait_ge(S("o_ready"), p + 1)
                for b2 in range(PB):
                    for f in range(C):
                        m = pe.matmul(ps[:, 7, b2 * D:(b2 + 1) * D], o_t[:, f, b2 * N:(b2 + 1) * N], w_o[:, f, :],
                                      start=(f == 0), stop=(f == C - 1))
                m.then_inc(S("y_done"), 1)

            def l1(g, first):
                qk(g, first)
                scores_wait(g, 0)
                scores(g, 0)
                if not first:
                    attend(g, 1, 2 * g - 1)
                for b in range(GB):
                    m = proj_n(ps[:, 4 + b // 2, (b % 2) * D:(b % 2 + 1) * D], b, v1_hi, v1_lo)
                m.then_inc(S("v1_done"), 1)
                scores_wait(g, 1)
                scores(g, 1)
                pe.wait_ge(S("v1_ready"), g + 1)
                turn(g + G + 1, 4)
                pe.wait_ge(ht_ready, g + G + 2)
                attend(g, 0, 2 * g)

            pe.wait_ge(S("nrm_ready"), G)
            pe.wait_ge(S("fin0"), G)
            l1(0, True)
            with pe.Fori(1, G - 1) as g:
                l1(g, False)
            l1(G - 1, False)
            attend(G, 1, NP - 1)

            def sum_rows(g):
                pe.wait_ge(hi_ready, g + 2 * G + 1)
                pe.wait_ge(S("e_ready"), g)
                for w in (s2_hi, s2_lo):
                    for c in range(C):
                        pe.matmul(ps[:, 4, :], w[:, c, :], h_hi[:, c, :], start=(w is s2_hi and c == 0), stop=False,
                                  skip_group_check=True)
                pe.wait_ge(lo_ready, g + 2 * G + 1)
                for c in range(C):
                    m = pe.matmul(ps[:, 4, :], s2_hi[:, c, :], h_lo[:, c, :], start=False, stop=(c == C - 1),
                                  skip_group_check=True)
                m.then_inc(S("s2_done"), 1)

            def project2(g):
                pe.wait_ge(S("h_ready"), g)
                if not (isinstance(g, int) and g < 2):
                    pe.wait_ge(S("fin2"), g - 1)
                for b in (2, 3, 0, 1):
                    m = proj_n(ps[:, b, 0:D + 2], b, w2_hi, w2_lo)
                m.then_inc(S("h_done"), 1)

            def turn_p2(g):
                pe.wait_ge(S("p2_ready"), g)
                for b in range(GB):
                    m = pe.transpose(ps[:, 7, b * N:(b + 1) * N], p2[:, b, :], ident[:])
                m.then_inc(S("p2_turned"), 1)

            def attend2(g, slot, last):
                pe.wait_ge(S("p2t_ready"), g)
                pe.wait_ge(S("h_ready"), g if last else g + 1)
                for b in range(GB):
                    m = pe.matmul(ps[:, b // 2, (b % 2) * D:(b % 2 + 1) * D], p2_t[:, b, :], vals[:, slot, b, :],
                                  start=True, stop=True)
                m.then_inc(S("att_done"), 1)

            def l2(g, slot, first, last):
                sum_rows(g)
                project2(g)
                if not first:
                    turn_p2(g)
                if not last:
                    turn(g + 2 * G + 1, 5)
                if not first:
                    attend2(g, 1 - slot, False)

            pe.wait_ge(S("fin1"), NP)
            l2(0, 0, True, False)
            l2(1, 1, False, False)
            with pe.Fori(0, (G - 4) // 2) as i:
                l2(2 * i + 2, 0, False, False)
                l2(2 * i + 3, 1, False, False)
            l2(G - 2, 0, False, False)
            l2(G - 1, 1, False, True)
            turn_p2(G)
            attend2(G, 1, True)

            def gather(g):
                pe.wait_ge(S("hn_ready"), g + 1)
                pe.wait_ge(S("a_lo_ready"), g)
                for b in range(GB):
                    for c in range(C):
                        m = pe.matmul(ps[:, c, b * N:(b + 1) * N],
                                      buf_a[:, :, :].rearrange("p c (b d) -> p (c b) d", d=D)[:, b, c * P:(c + 1) * P],
                                      norm_adj_t[:], start=True, stop=True)
                m.then_inc(S("a_done"), 1)

            def project3(g, slot):
                pe.wait_ge(S("a_lo_ready"), g + 1)
                if not (isinstance(g, int) and g == 0):
                    pe.wait_ge(S("fin3"), g)
                for b in range(GB):
                    cols = slice(b * N, (b + 1) * N)
                    m = split3(ps[:, 2 + b // 2, (b % 2) * D:(b % 2 + 1) * D],
                               (lambda c: a_hi[:, slot, c, cols], lambda c: a_lo[slot][:, c, cols]),
                               (lambda c: w3_hi[:, c, :], lambda c: w3_lo[:, c, :]), "all")
                m.then_inc(S("out3_done"), 1)

            pe.wait_ge(S("fin2"), G)
            gather(0)
            gather(1)
            project3(0, 0)
            with pe.Fori(0, (G - 2) // 2) as i:
                for k in range(2):
                    gather(2 * i + k + 2)
                    project3(2 * i + k + 1, 1 - k)
            project3(G - 1, 1)

        @block.vector
        def _(dve):
            def stats(n, g, ready, count):
                dve.wait_ge(ready, count)
                for b in range(GB):
                    i = dve.bn_stats(st[:, b, :], xg(g, b, 1))
                i.then_inc(bn_done, 1)
                dve.wait_ge(bn_done, n + 1)
                dve.tensor_copy(st_seen[:], st[:, 0, 0:1])
                for b in range(GB):
                    i = dve.bn_aggr(mv[:, b, :], st[:, b, :])
                i.then_inc(stat_ready, 1)

            def shift(n):
                dve.wait_ge(rstd_ready, n + 1)
                dve.scalar_tensor_tensor(nmr[:], mv[:, :, 0], -1.0, rstd[:], ALU.mult, ALU.mult).then_inc(nmr_ready, 1)

            def normalise(n, g):
                shift(n)
                dve.wait_ge(nmr_ready, n + 1)
                dve.wait_ge(turned, n)
                for b in range(GB):
                    i = dve.tensor_scalar(xn[:, b, :], xg(g, b, 1), rstd[:, b:b + 1], nmr[:, b:b + 1],
                                          ALU.mult, ALU.add)
                i.then_inc(xn_ready, 1)

            def hi_part(n):
                dve.wait_ge(ht_ready, n + 1)
                dve.tensor_copy(h_hi[:], h_t[:]).then_inc(hi_ready, 1)

            dve.wait_ge(w_in, 16 * NLOAD)
            dve.wait_ge(su_pool, 1)
            stats(0, 0, x_in, 16)
            own = [0]

            def mine(i):
                own[0] += 1
                i.then_inc(S("su_own"), 1)
                dve.wait_ge(S("su_own"), own[0])

            dve.tensor_reduce(deg[:], adj_n[:], AX_X, ALU.add).then_inc(S("deg_ready"), 1)
            normalise(0, 0)
            dve.tensor_scalar(maskb[:], adj_n[:], -1.0, BIG, ALU.add, ALU.mult)
            dve.tensor_scalar(beta_i[:], ident[:], beta_c[:, 0:1], None, ALU.mult)
            dve.tensor_scalar(b3_row[:], b3_row[:], -1.0, None, ALU.add)
            dve.tensor_scalar(bqs_c[:], bq_c[:], float(HD) ** -0.5, None, ALU.mult)
            for c in range(C):
                dve.tensor_scalar(bv_rep[:, c, :], ones[:], bv_c[:, c:c + 1], None, ALU.mult)
            dve.wait_ge(S("dis_ready"), 1)
            mine(dve.tensor_scalar(deg_pos[:], deg[:], 0.0, None, ALU.is_gt))
            mine(dve.tensor_tensor(dis[:], deg_pow[:], deg_pos[:], ALU.mult))
            dve.tensor_scalar(adj_s[:], adj_n[:], dis[:, 0:1], None, ALU.mult).then_inc(su_dve, 1)

            def split(hi, lo, src):
                mine(dve.tensor_copy(hi, src))
                dve.tensor_tensor(lo, src, f32(hi), ALU.subtract)

            hi_part(0)
            dve.wait_ge(su_pe, 1)
            split(m_hi[:], m_lo[:], ps[:, 0:2, 0:D])
            split(v0_hi[:], v0_lo[:], ps[:, 2:4, 0:D])
            for i, (hi, lo) in enumerate(((q1_hi, q1_lo), (k1_hi, k1_lo), (v1_hi, v1_lo), (w3_hi, w3_lo))):
                split(hi[:], lo[:], wstage[:, i])
            for c in range(C):
                for t in range(2):
                    mine(dve.tensor_tensor(w2junk[:], w2x[:, c, 0:D], a_row[:, t, :], ALU.mult))
                    mine(dve.tensor_reduce(w2c[:, c, t:t + 1], w2junk[:], AX_X, ALU.add))
            for c in range(C):
                dve.tensor_copy(w2x[:, c, D:D + 2], w2c[:, c, 0:1].broadcast_to([P, 2]))
                mine(dve.tensor_scalar(w2rep[:, c, :], ones[:], w2c[:, c, 1:2], None, ALU.mult))
            split(w2_hi[:], w2_lo[:], w2x[:])
            split(s2_hi[:], s2_lo[:], w2rep[:])
            dve.wait_ge(su_pe, 2)
            dve.tensor_scalar(norm_adj_t[:], ps[:, 4, 0:N], dis[:, 0:1], None, ALU.mult)
            dve.tensor_tensor(bo_row[:], ps[:, 7, 0:D], bo_row[:], ALU.add).then_inc(su_dve, 1)

            def l0(g, stats_args):
                stats(g + 1, *stats_args)
                normalise(g + 1, stats_args[0])
                dve.wait_ge(S("rel_done"), g + 1)
                dve.tensor_tensor(rel[:].rearrange("p (b n) -> p b n", b=GB),
                                  ps[:, 4, :].rearrange("p (b n) -> p b n", b=GB),
                                  bc(adj_n[:], GB), ALU.mult).then_inc(S("rel_ready"), 1)
                hi_part(g + 1)
                dve.wait_ge(S("nrm_done"), g + 1)
                dve.tensor_copy(nrm[:], ps[:, 7, 0:GB]).then_inc(S("nrm_ready"), 1)
                dve.wait_ge(S("out0_done"), g + 1)
                dve.wait_ge(S("rnrm_ready"), g + 1)
                for b in range(GB):
                    i = dve.scalar_tensor_tensor(xg(g, b, 1), ps[:, 2 + b // 2, (b % 2) * D:(b % 2 + 1) * D],
                                                 rnrm[:, b:b + 1], xg(g, b, 1), ALU.mult, ALU.add)
                i.then_inc(S("fin0"), 1)

            with dve.Fori(0, G - 1) as g:
                l0(g, (g + 1, x_in, g * 16 + 32))
            l0(G - 1, (0, S("fin0"), 1))

            def mask_max(g, half):
                p = 2 * g + half
                dve.wait_ge(S("s_done"), p + 1)
                for b2 in range(PB):
                    if not (isinstance(g, int) and 2 * p + b2 < 2):
                        dve.wait_ge(S("shifted"), 2 * p + b2 - 1)
                    for f in range(C):
                        o = b2 * C * N + f * N
                        i = dve.tensor_tensor(sc[:, b2, :, f, :], ps[:, 0:R, o:o + N], bc(maskb[:], R), ALU.add)
                    i.then_inc(S("masked"), 1)
                    dve.wait_ge(S("masked"), 2 * p + b2 + 1)
                    dve.tensor_reduce(mx[:, b2, :], sc[:, b2].rearrange("p r f n -> p (r f) n"), AX_X,
                                      ALU.max).then_inc(S("max_ready"), 1)

            def sum_probs(p, half):
                for b2 in range(PB):
                    dve.wait_ge(S("exp_ready"), 2 * p + b2 + 1)
                    i = dve.tensor_reduce(sums[:, b2], pr[:, half, b2].rearrange("p r f n -> p f r n"), AX_X, ALU.add)
                i.then_inc(S("sums_own"), 1)
                dve.wait_ge(S("sums_own"), p + 1)
                dve.wait_ge(S("spread"), p)
                dve.reciprocal(rinv[:].rearrange("p b f r -> p (b f r)"),
                               sums[:].rearrange("p b f r -> p (b f r)")).then_inc(S("rinv_ready"), 1)

            def weigh(p):
                dve.wait_ge(S("pv_done"), p + 1)
                dve.wait_ge(S("rt_ready"), p + 1)
                dve.tensor_tensor(o_t[:].rearrange("p c n -> p (c n)"), ps[:, 6, :],
                                  rinv_t[:].rearrange("p c n -> p (c n)"), ALU.mult).then_inc(S("o_ready"), 1)

            def add1(g, half, p):
                dve.wait_ge(S("y_done"), p + 1)
                dve.wait_ge(S("bias1"), g + 1)
                dve.tensor_tensor(xg(g, PB * half, PB), ps[:, 7, :], xg(g, PB * half, PB), ALU.add)\
                   .then_inc(S("fin1"), 1)

            def l1(g, first, stats_args):
                if not first:
                    sum_probs(2 * g - 1, 1)
                mask_max(g, 0)
                if not first:
                    weigh(2 * g - 1)
                    add1(g - 1, 1, 2 * g - 1)
                stats(g + G + 1, *stats_args)
                normalise(g + G + 1, stats_args[0])
                sum_probs(2 * g, 0)
                mask_max(g, 1)
                hi_part(g + G + 1)
                weigh(2 * g)
                add1(g, 0, 2 * g)

            l1(0, True, (1, S("fin0"), G))
            with dve.Fori(1, G - 1) as g:
                l1(g, False, (g + 1, S("fin0"), G))
            l1(G - 1, False, (0, S("fin1"), 2))
            sum_probs(NP - 1, 1)
            weigh(NP - 1)
            add1(G - 1, 1, NP - 1)

            def edges(g):
                dve.wait_ge(S("s2_done"), g + 1)
                dve.wait_ge(S("s1_ready"), g + 1)
                dve.wait_ge(S("shifted2"), g)
                dve.tensor_tensor(e2[:], ps[:, 4, :].rearrange("p (b n) -> p b n", b=GB), bcol(s1[:], N),
                                  ALU.add).then_inc(S("e_ready"), 1)
                dve.wait_ge(S("e_ready"), g + 1)
                dve.scalar_tensor_tensor(e2[:], e2[:], ALPHA, e2[:], ALU.mult, ALU.max).then_inc(S("lr_own"), 1)
                dve.wait_ge(S("lr_own"), g + 1)
                dve.tensor_tensor(e2[:], e2[:], bc(adj_n[:], GB), ALU.mult).then_inc(S("em_own"), 1)
                dve.wait_ge(S("em_own"), g + 1)
                dve.tensor_reduce(mx2[:], e2[:], AX_X, ALU.max).then_inc(S("max2_ready"), 1)

            def sum_probs2(g):
                dve.wait_ge(S("exp2_ready"), g + 1)
                dve.tensor_reduce(sum2[:], p2[:], AX_X, ALU.add).then_inc(S("sum2_own"), 1)
                dve.wait_ge(S("sum2_own"), g + 1)
                dve.reciprocal(ri2[:], sum2[:]).then_inc(S("ri2_ready"), 1)

            def add_beta(g):
                dve.wait_ge(S("p2_turned"), g)
                dve.tensor_tensor(p2_t[:], ps[:, 7, :].rearrange("p (b n) -> p b n", b=GB), bc(beta_i[:], GB),
                                  ALU.add).then_inc(S("p2t_ready"), 1)

            def add2(g):
                dve.wait_ge(S("ey_ready"), g)
                dve.scalar_tensor_tensor(xg(g - 1), ps[:, 0:2, :].rearrange("p a n -> p (a n)"), 0.0, xg(g - 1),
                                         ALU.max, ALU.add).then_inc(S("r_own"), 1)
                dve.wait_ge(S("r_own"), g)
                dve.scalar_tensor_tensor(xg(g - 1), buf_b[:].rearrange("p c n -> p (c n)"), 1.0, xg(g - 1),
                                         ALU.min, ALU.add).then_inc(S("fin2"), 1)

            def l2(g, first, stats_args):
                stats(g + 2 * G + 1, *stats_args)
                if not (isinstance(g, int) and g == G - 1):
                    normalise(g + 2 * G + 1, stats_args[0])
                else:
                    shift(g + 2 * G + 1)
                if not first:
                    add_beta(g)
                edges(g)
                if not (isinstance(g, int) and g == G - 1):
                    hi_part(g + 2 * G + 1)
                if not first:
                    add2(g)
                sum_probs2(g)

            l2(0, True, (1, S("fin1"), NP))
            with dve.Fori(1, G - 1) as g:
                l2(g, False, (g + 1, S("fin1"), NP))
            l2(G - 1, False, (0, S("fin2"), 1))
            add_beta(G)
            add2(G)

            def lo3(g, slot):
                dve.wait_ge(S("a_hi_ready"), g + 1)
                dve.tensor_tensor(a_lo[slot][:], ps[:, 0:2, :], f32(a_hi[:, slot]), ALU.subtract)\
                   .then_inc(S("a_lo_ready"), 1)

            def add3(g):
                dve.wait_ge(S("out3_done"), g + 1)
                dve.wait_ge(S("bias3"), g + 1)
                dve.tensor_tensor(xg(g), ps[:, 2:4, :].rearrange("p a n -> p (a n)"), xg(g), ALU.add)\
                   .then_inc(S("fin3"), 1)

            def stage3(g):
                stats(g + 3 * G, g, S("fin2"), G)
                dve.wait_ge(S("hn_ready"), g)
                shift(g + 3 * G)

            stage3(1)
            lo3(0, 0)
            with dve.Fori(0, (G - 2) // 2) as i:
                for k in range(2):
                    stage3(2 * i + k + 2)
                    lo3(2 * i + k + 1, 1 - k)
                    add3(2 * i + k)
            lo3(G - 1, 1)
            add3(G - 2)
            add3(G - 1)

        @block.scalar
        def _(act):
            def h_part(n, bank):
                act.wait_ge(turned, n + 1)
                act.activation(h_t[:], ps[:, bank:bank + 2, :], ACT.Relu).then_inc(ht_ready, 1)

            h_part(0, 5)

            def l0(g):
                act.wait_ge(S("g_done"), g + 1)
                act.activation(buf_a[:], ps[:, 0:2, :], ACT.Copy).then_inc(S("gt_ready"), 1)
                act.wait_ge(S("v_done"), g + 1)
                act.activation(vals[:, 0].rearrange("p b d -> p (b d)"),
                               ps[:, 2:4, :].rearrange("p a n -> p (a n)"), ACT.Copy).then_inc(S("v_ready"), 1)
                h_part(g + 1, 5)

            with act.Fori(0, G) as g:
                l0(g)

            def take_turned(p):
                act.wait_ge(S("rinv_ready"), p + 1)
                act.wait_ge(S("rt_done"), p)
                act.activation(rinv_x[:].rearrange("p b f (r d) -> p (b f r) d", d=HD),
                               rinv[:].rearrange("p b f r -> p (b f r)").unsqueeze(2).broadcast_to([P, PB * C * R, HD]),
                               ACT.Copy).then_inc(S("spread"), 1)
                act.wait_ge(S("rt_done"), p + 1)
                act.activation(rinv_t[:].rearrange("p c n -> p (c n)"), ps[:, 7, :], ACT.Copy)\
                   .then_inc(S("rt_ready"), 1)
                for j in range(PB * C):
                    act.wait_ge(S("pt_done"), 4 * p + j + 1)
                    act.activation(pr_t[:, j % 2].rearrange("p r n -> p (r n)"), ps[:, 4 + j % C, :], ACT.Copy)\
                       .then_inc(S("pt_ready"), 1)

            def exponent(p, half, b2):
                act.wait_ge(S("shifted"), 2 * p + b2 + 1)
                t = pr[:, half, b2].rearrange("p r f n -> p (r f n)")
                act.activation(t, t, ACT.Exp).then_inc(S("exp_ready"), 1)

            def l1(g, first):
                act.wait_ge(S("q_done"), g + 1)
                for f in range(C):
                    i = act.activation(buf_a[:, f, :], ps[:, 4 + f, :], ACT.Identity, bias=bqs_c[:, f:f + 1],
                                       scale=float(HD) ** -0.5)
                i.then_inc(S("q_ready"), 1)
                act.wait_ge(S("k_done"), g + 1)
                for f in range(C):
                    i = act.activation(buf_b[:, f, :], ps[:, 6 + f, :], ACT.Identity, bias=bk_c[:, f:f + 1])
                i.then_inc(S("k_ready"), 1)
                if not first:
                    take_turned(2 * g - 1)
                exponent(2 * g, 0, 0)
                act.wait_ge(S("v1_done"), g + 1)
                act.activation(vals[:, 0].rearrange("p b d -> p (b d)"),
                               ps[:, 4:6, :].rearrange("p a n -> p (a n)"), ACT.Copy).then_inc(S("v1_ready"), 1)
                exponent(2 * g, 0, 1)
                h_part(g + G + 1, 4)
                take_turned(2 * g)
                exponent(2 * g + 1, 1, 0)
                exponent(2 * g + 1, 1, 1)

            act.wait_ge(su_dve, 2)
            l1(0, True)
            with act.Fori(1, G) as g:
                l1(g, False)
            take_turned(NP - 1)

            def take_h(g, slot):
                act.wait_ge(S("h_done"), g + 1)
                act.wait_ge(S("e_ready"), g)
                act.activation(s1[:], ps[:, 0:GB, D], ACT.Copy).then_inc(S("s1_ready"), 1)
                act.activation(vals[:, slot], ps[:, 0:GB, 0:D], ACT.Copy).then_inc(S("h_ready"), 1)

            def exponent2(g):
                act.wait_ge(S("shifted2"), g + 1)
                act.activation(p2[:], p2[:], ACT.Exp).then_inc(S("exp2_ready"), 1)

            def exp_y(g):
                act.wait_ge(S("att_done"), g)
                act.activation(buf_b[:], ps[:, 0:2, :], ACT.Exp).then_inc(S("ey_ready"), 1)

            def natural(g):
                act.wait_ge(nmr_ready, g + 3 * G + 1)
                act.wait_ge(S("a_done"), g)
                for b in range(GB):
                    i = act.activation(buf_a[:].rearrange("p c (b d) -> p (c b) d", d=D)[:, b, :], xg(g, b, 1),
                                       ACT.Relu, bias=nmr[:, b:b + 1], scale=rstd[:, b:b + 1])
                i.then_inc(S("hn_ready"), 1)

            def l2(g, slot, first):
                take_h(g, slot)
                if not (isinstance(g, int) and g == G - 1):
                    h_part(g + 2 * G + 1, 5)
                if not first:
                    exp_y(g)
                exponent2(g)

            act.wait_ge(S("fin1"), NP)
            l2(0, 0, True)
            with act.Fori(0, (G - 2) // 2) as i:
                l2(2 * i + 1, 1, False)
                l2(2 * i + 2, 0, False)
            l2(G - 1, 1, False)
            natural(0)
            exp_y(G)

            def hi3(g, slot):
                act.wait_ge(S("a_done"), g + 1)
                act.activation(a_hi[:, slot], ps[:, 0:2, :], ACT.Copy).then_inc(S("a_hi_ready"), 1)

            hi3(0, 0)
            natural(1)
            with act.Fori(0, (G - 2) // 2) as i:
                for k in range(2):
                    hi3(2 * i + k + 1, 1 - k)
                    natural(2 * i + k + 2)
            hi3(G - 1, 1)

        @block.gpsimd
        def _(pool):
            def minus_half(n_cols):
                return expo[:, 0:n_cols]

            def rstd_part(n):
                pool.wait_ge(stat_ready, n + 1)
                pool.tensor_tensor(veps[:], mv[:, :, 1], eps_c[:], ALU.add).then_inc(veps_done, 1)
                pool.wait_ge(veps_done, n + 1)
                pool.tensor_tensor(rstd[:], veps[:], minus_half(GB), ALU.pow).then_inc(rstd_ready, 1)

            def lo_part(n):
                pool.wait_ge(hi_ready, n + 1)
                pool.tensor_tensor(h_lo[:], h_t[:], f32(h_hi[:]), ALU.subtract).then_inc(lo_ready, 1)

            pool.memset(ones[:], 1.0)
            pool.memset(expo[:], -0.5)
            pool.memset(eps_c[:], EPS)
            pool.memset(ident[:], 0.0).then_inc(S("su_zero"), 1)
            pool.wait_ge(S("su_zero"), 1)
            pool.affine_select(out=ident[:], in_=ident[:], compare_op=ALU.not_equal, fill=1.0, base=0,
                               pattern=[[-1, P]], channel_multiplier=1).then_inc(su_pool, 1)
            pool.wait_ge(su_pool, 1)
            rstd_part(0)
            pool.wait_ge(S("deg_ready"), 1)
            pool.tensor_scalar(deg_safe[:], deg[:], TINY, None, ALU.max).then_inc(S("dis_own"), 1)
            pool.wait_ge(S("dis_own"), 1)
            pool.tensor_tensor(deg_pow[:], deg_safe[:], minus_half(1), ALU.pow).then_inc(S("dis_ready"), 1)
            lo_part(0)

            with pool.Fori(0, G) as g:
                rstd_part(g + 1)
                pool.wait_ge(S("rel_ready"), g + 1)
                pool.tensor_tensor(rel2[:], rel[:], rel[:], ALU.mult).then_inc(S("rel2_ready"), 1)
                pool.wait_ge(S("nrm_ready"), g + 1)
                pool.tensor_tensor(rnrm[:], nrm[:], minus_half(GB), ALU.pow).then_inc(S("rnrm_ready"), 1)
                lo_part(g + 1)

            pool.wait_ge(su_dve, 2)

            def shift_scores(g, half):
                p = 2 * g + half
                for b2 in range(PB):
                    pool.wait_ge(S("max_ready"), 2 * p + b2 + 1)
                    if not (isinstance(g, int) and p < 2):
                        pool.wait_ge(S("fin1"), p - 1)
                    pool.tensor_tensor(pr[:, half, b2].rearrange("p r f n -> p (r f) n"),
                                       sc[:, b2].rearrange("p r f n -> p (r f) n"), bcol(mx[:, b2, :], N),
                                       ALU.subtract).then_inc(S("shifted"), 1)

            def l1(g):
                shift_scores(g, 0)
                rstd_part(g + G + 1)
                pool.wait_ge(xn_ready, g + G + 1)
                pool.wait_ge(S("fin0"), g + 1)
                pool.tensor_tensor(xg(g).rearrange("p (b d) -> p b d", b=GB), xg(g).rearrange("p (b d) -> p b d", b=GB),
                                   bo_row[:].unsqueeze(1).broadcast_to([P, GB, D]), ALU.add).then_inc(S("bias1"), 1)
                shift_scores(g, 1)
                lo_part(g + G + 1)

            l1(0)
            with pool.Fori(1, G) as g:
                l1(g)

            def l2(g):
                rstd_part(g + 2 * G + 1)
                pool.wait_ge(S("max2_ready"), g + 1)
                if not (isinstance(g, int) and g == 0):
                    pool.wait_ge(S("p2_turned"), g)
                pool.tensor_tensor(p2[:], e2[:], bcol(mx2[:], N), ALU.subtract).then_inc(S("shifted2"), 1)
                if not (isinstance(g, int) and g == G - 1):
                    lo_part(g + 2 * G + 1)
                pool.wait_ge(S("ri2_ready"), g + 1)
                pool.tensor_tensor(p2[:], p2[:], bcol(ri2[:], N), ALU.mult).then_inc(S("p2_ready"), 1)

            l2(0)
            with pool.Fori(1, G - 1) as g:
                l2(g)
            l2(G - 1)

            def bias3(g):
                pool.wait_ge(S("hn_ready"), g + 1)
                pool.tensor_tensor(xg(g).rearrange("p (b d) -> p b d", b=GB), xg(g).rearrange("p (b d) -> p b d", b=GB),
                                   b3_row[:].unsqueeze(1).broadcast_to([P, GB, D]), ALU.add).then_inc(S("bias3"), 1)

            pool.wait_ge(S("hn_ready"), 1)
            rstd_part(3 * G + 1)
            bias3(0)
            with pool.Fori(2, G) as g:
                pool.wait_ge(S("hn_ready"), g)
                rstd_part(g + 3 * G)
                bias3(g - 1)
            bias3(G - 1)


_INS = ['x', 'adj', 'L0_gnn_Wq', 'L0_gnn_Wk', 'L0_gnn_Wv', 'L1_gnn_Wq', 'L1_gnn_bq', 'L1_gnn_Wk', 'L1_gnn_bk',
        'L1_gnn_Wv', 'L1_gnn_bv', 'L1_gnn_Wo', 'L1_gnn_bo', 'L2_gnn_W', 'L2_gnn_a', 'L2_gnn_beta',
        'L3_gnn_weight', 'L3_gnn_bias']
_OUTS = [((64, 128, 256), 'float32')]


def kernel(**inputs):
    import numpy as _np
    import concourse.bacc as _bacc
    from concourse import mybir as _mybir
    from concourse.bass_utils import run_bass_kernel_spmd as _run

    nc = _bacc.Bacc("TRN2", target_bir_lowering=False, num_devices=1)
    arrays, args = {}, []
    for name in _INS:
        a = _np.ascontiguousarray(inputs[name])
        arrays[f"in_{name}_dram"] = a
        args.append(nc.dram_tensor(f"in_{name}_dram", a.shape, _mybir.dt.from_np(a.dtype), kind="ExternalInput").ap())
    for i, (shape, dtype) in enumerate(_OUTS):
        dt = _mybir.dt.from_np(_np.dtype(dtype))
        args.append(nc.dram_tensor(f"out_{i}_dram", shape, dt, kind="ExternalOutput").ap())
    four_layer_graph_kernel(nc, *args)
    r = _run(nc, [arrays], core_ids=[0])
    got = tuple(r.results[0][f"out_{i}_dram"] for i in range(len(_OUTS)))
    return got[0]
```

```python
from contextlib import ExitStack

import concourse.bass as bass
from concourse import mybir

ALU = mybir.AluOpType
ACT = mybir.ActivationFunctionType
F32 = mybir.dt.float32
F32R = mybir.dt.float32r
AX_X = mybir.AxisListType.X


def four_layer_graph_kernel(nc, x, adj, L0_gnn_Wq, L0_gnn_Wk, L0_gnn_Wv,
                            L1_gnn_Wq, L1_gnn_bq, L1_gnn_Wk, L1_gnn_bk, L1_gnn_Wv, L1_gnn_bv,
                            L1_gnn_Wo, L1_gnn_bo, L2_gnn_W, L2_gnn_a, L2_gnn_beta,
                            L3_gnn_weight, L3_gnn_bias, out):
    B, N, D = x.shape
    P = 128
    GB = 4
    G = B // GB
    C = D // P
    GN = GB * N
    GD = GB * D
    H = 8
    HD = D // H
    R = P // HD
    PB = 2
    NP = B // PB
    EPS = 1e-05
    ALPHA = 0.2
    BIG = 1000000000.0
    TINY = 1e-30
    assert N == P and GN == 512 and C == 2 and R == 4

    ctx = ExitStack()
    with ctx:
        def sb(name, shape, dt=F32):
            return ctx.enter_context(nc.sbuf_tensor(name, shape, dt))

        def sem(name):
            return ctx.enter_context(nc.semaphore(name))

        ps = ctx.enter_context(nc.psum_tensor("ps", [P, 8, 512], F32))

        xs = sb("xs", [P, B * D])
        adj_n = sb("adj_n", [P, N])
        ident = sb("ident", [P, P])
        ones = sb("ones", [P, P])
        maskb = sb("maskb", [P, N])
        beta_i = sb("beta_i", [P, N])
        beta_c = sb("beta_c", [P, 1])
        deg = sb("deg", [P, 1])
        deg_pos = sb("deg_pos", [P, 1])
        deg_safe = sb("deg_safe", [P, 1])
        deg_pow = sb("deg_pow", [P, 1])
        dis = sb("dis", [P, 1])
        adj_s = sb("adj_s", [P, N])
        norm_adj_t = sb("norm_adj_t", [P, N])
        expo = sb("expo", [P, GB])
        eps_c = sb("eps_c", [P, GB])
        bo_row = sb("bo_row", [P, D])
        b3_row = sb("b3_row", [P, D])
        bq_c = sb("bq_c", [P, C])
        bqs_c = sb("bqs_c", [P, C])
        bk_c = sb("bk_c", [P, C])
        bv_c = sb("bv_c", [P, C])
        bv_rep = sb("bv_rep", [P, C, P])
        a_row = sb("a_row", [P, 2, D])
        wq0 = sb("wq0", [P, C, D])
        wk0 = sb("wk0", [P, C, D])
        wv0 = sb("wv0", [P, C, D])
        wstage = sb("wstage", [P, 4, C * D])
        w_o = sb("w_o", [P, C, D])
        w2x = sb("w2x", [P, C, D + 2])
        w2c = sb("w2c", [P, C, 2])
        w2junk = sb("w2junk", [P, D])
        w2rep = sb("w2rep", [P, C, P])
        m_hi, m_lo = sb("m_hi", [P, C, D], F32R), sb("m_lo", [P, C, D], F32R)
        v0_hi, v0_lo = sb("v0_hi", [P, C, D], F32R), sb("v0_lo", [P, C, D], F32R)
        q1_hi, q1_lo = sb("q1_hi", [P, C, D], F32R), sb("q1_lo", [P, C, D], F32R)
        k1_hi, k1_lo = sb("k1_hi", [P, C, D], F32R), sb("k1_lo", [P, C, D], F32R)
        v1_hi, v1_lo = sb("v1_hi", [P, C, D], F32R), sb("v1_lo", [P, C, D], F32R)
        o1_hi, o1_lo = sb("o1_hi", [P, C, D], F32R), sb("o1_lo", [P, C, D], F32R)
        w3_hi, w3_lo = sb("w3_hi", [P, C, D], F32R), sb("w3_lo", [P, C, D], F32R)
        w2_hi, w2_lo = sb("w2_hi", [P, C, D + 2], F32R), sb("w2_lo", [P, C, D + 2], F32R)
        s2_hi, s2_lo = sb("s2_hi", [P, C, P], F32R), sb("s2_lo", [P, C, P], F32R)
        st = sb("st", [P, GB, 6])
        st_seen = sb("st_seen", [P, 1])
        mv = sb("mv", [P, GB, 2])
        neg_mean = sb("neg_mean", [P, GB])
        veps = sb("veps", [P, GB])
        rstd = sb("rstd", [P, GB])
        nmr = sb("nmr", [P, GB])
        xn = sb("xn", [P, GB, D])
        h_t = sb("h_t", [P, C, GN])
        h_hi = sb("h_hi", [P, C, GN], F32R)
        h_lo = sb("h_lo", [P, C, GN], F32R)
        buf_a = sb("buf_a", [P, C, GN])
        buf_b = sb("buf_b", [P, C, GN])
        vals = sb("vals", [P, 2, GB, D])
        rel = sb("rel", [P, GN])
        rel2 = sb("rel2", [P, GN])
        nrm = sb("nrm", [P, GB])
        rnrm = sb("rnrm", [P, GB])
        sc = wstage[:].rearrange("p (b r) m -> p (b r m)", b=PB).rearrange(
            "p (b r f n) -> p b r f n", b=PB, r=R, f=C)
        mx = sb("mx", [P, PB, R * C])
        pr = sb("pr", [P, 2, PB, R, C, N])
        sums = sb("sums", [P, PB, R * C])
        rinv = sb("rinv", [P, PB, R * C])
        pr_t = sb("pr_t", [P, 2, R, N])
        o_hi = sb("o_hi", [P, C, PB * N], F32R)
        o_lo = sb("o_lo", [P, C, PB * N], F32R)
        s1 = sb("s1", [P, GB])
        e2 = sb("e2", [P, GB, N])
        p2 = sb("p2", [P, GB, N])
        p2_t = sb("p2_t", [P, GB, N])
        mx2 = sb("mx2", [P, GB])
        sum2 = sb("sum2", [P, GB])
        ri2 = sb("ri2", [P, GB])
        a_hi = sb("a_hi", [P, 2, C, GN], F32R)
        a_lo = (h_hi, h_lo)

        sems = {}

        def S(name):
            if name not in sems:
                sems[name] = sem(name)
            return sems[name]

        w_in, w_in2, x_in, x_out = S("w_in"), S("w_in2"), S("x_in"), S("x_out")
        su_pool, su_dve, su_pe, su_hi, su_lo = S("su_pool"), S("su_dve"), S("su_pe"), S("su_hi"), S("su_lo")
        bn_done, stat_ready, veps_done = S("bn_done"), S("stat_ready"), S("veps_done")
        rstd_done, nmr_ready = S("rstd_done"), S("nmr_ready")
        xn_ready, turned, ht_ready, hi_ready, lo_ready = S("xn_ready"), S("turned"), S("ht_ready"), S("hi_ready"), S("lo_ready")

        def xg(g, b=0, nb=GB):
            return xs[:, bass.ds(g * GD + b * D, nb * D)]

        def bc(ap, reps):
            return ap.unsqueeze(1).broadcast_to([P, reps, N])

        def bcol(ap, cols):
            return ap.unsqueeze(2).broadcast_to([P, ap.shape[1], cols])

        def flat(ap):
            return ap.rearrange("p a n -> p (a n)")

        def f32(ap):
            return ap.bitcast(F32)

        def rows(w):
            return w.rearrange("(c p) f -> p c f", p=P)

        loads = [(wq0[:], rows(L0_gnn_Wq)), (wk0[:], rows(L0_gnn_Wk)), (wv0[:], rows(L0_gnn_Wv)), (adj_n[:], adj)]
        loads2 = [(t[:], v.rearrange("(c p) -> p c", p=P)) for t, v in
                  ((bq_c, L1_gnn_bq), (bk_c, L1_gnn_bk), (bv_c, L1_gnn_bv))]
        loads2 += [(t[:], v.partition_broadcast(P)) for t, v in
                   ((bo_row, L1_gnn_bo), (b3_row, L3_gnn_bias), (beta_c, L2_gnn_beta))]
        loads2 += [(w_o[:], rows(L1_gnn_Wo))]
        loads2 += [(wstage[:, i].rearrange("p (c f) -> p c f", c=C), rows(w))
                   for i, w in enumerate((L1_gnn_Wq, L1_gnn_Wk, L1_gnn_Wv, L3_gnn_weight))]
        loads2 += [(w2x[:, :, 0:D], rows(L2_gnn_W))]
        loads2 += [(a_row[:], L2_gnn_a.rearrange("(t f) o -> (o t) f", t=2).partition_broadcast(P))]
        staged = [(q1_hi, q1_lo), (k1_hi, k1_lo), (v1_hi, v1_lo), (w3_hi, w3_lo)]

        block = ctx.enter_context(nc.Block())

        @block.sync
        def _(sp):
            def load_x(g):
                sp.dma_start(xg(g).rearrange("p (b d) -> p b d", b=GB),
                             x[bass.ds(g * GB, GB)].rearrange("b n d -> n b d")).then_inc(x_in, 16)

            load_x(0)
            with nc.allow_non_contiguous_dma(reason="bias columns"):
                for dst, src in loads:
                    sp.dma_start(dst, src).then_inc(w_in, 16)
                sp.wait_ge(x_in, 16)
                load_x(1)
                for dst, src in loads2:
                    sp.dma_start(dst, src).then_inc(w_in2, 16)
            with sp.Fori(2, G) as g:
                sp.wait_ge(x_in, g * 16)
                load_x(g)
            with sp.Fori(0, G) as g:
                sp.wait_ge(S("fin3"), g + 1)
                sp.dma_start(out[bass.ds(g * GB, GB)].rearrange("b n d -> n b d"),
                             xg(g).rearrange("p (b d) -> p b d", b=GB)).then_inc(x_out, 16)
            sp.wait_ge(x_out, 16 * G)

        @block.tensor
        def _(pe):
            def proj_t(bank, w_hi, w_lo, part):
                h = h_hi if part == "hi" else h_lo
                for f in range(C):
                    for w in ((w_hi, w_lo) if part == "hi" else (w_hi,)):
                        for c in range(C):
                            m = pe.matmul(ps[:, bank + f, :], w[:, c, f * P:(f + 1) * P], h[:, c, :],
                                          start=(part == "hi" and w is w_hi and c == 0),
                                          stop=(part == "lo" and c == C - 1), skip_group_check=True)
                return m

            def proj_n(o, hs, cols, w_hi, w_lo):
                for i, (h, w) in enumerate(((hs[0], w_hi), (hs[0], w_lo), (hs[1], w_hi))):
                    for c in range(C):
                        m = pe.matmul(o, h[:, c, cols], w[:, c, :], start=(i == 0 and c == 0),
                                      stop=(i == 2 and c == C - 1), skip_group_check=True)
                return m

            def nodes(b):
                return slice(b * N, (b + 1) * N)

            def half_bank(bank, b):
                return ps[:, bank + b // 2, (b % 2) * D:(b % 2 + 1) * D]

            def turn(n, bank):
                pe.wait_ge(xn_ready, n + 1)
                for c in range(C):
                    for b in range(GB):
                        m = pe.transpose(ps[:, bank + c, nodes(b)], xn[:, b, c * P:(c + 1) * P], ident[:])
                m.then_inc(turned, 1)

            pe.wait_ge(su_pool, 1)
            pe.wait_ge(w_in, 16 * len(loads))
            for dc in range(C):
                for ec in range(C):
                    m = pe.matmul(ps[:, dc, 0:D], wq0[:, ec, dc * P:(dc + 1) * P], wk0[:, ec, :],
                                  start=(ec == 0), stop=(ec == C - 1))
            for dc in range(C):
                for ec in range(C):
                    m = pe.transpose(ps[:, 2 + dc, ec * P:(ec + 1) * P], wv0[:, ec, dc * P:(dc + 1) * P], ident[:])
            m.then_inc(su_pe, 1)
            turn(0, 5)
            pe.wait_ge(su_dve, 1)

            def l0(g, first):
                pe.wait_ge(hi_ready, g + 1)
                proj_t(0, m_hi, m_lo, "hi")
                pe.wait_ge(lo_ready, g + 1)
                proj_t(0, m_hi, m_lo, "lo").then_inc(S("g_done"), 1)
                if not first:
                    pe.wait_ge(S("fin0"), g)
                for b in range(GB):
                    m = proj_n(half_bank(2, b), (h_hi, h_lo), nodes(b), v0_hi, v0_lo)
                m.then_inc(S("v_done"), 1)
                pe.wait_ge(S("gt_ready"), g + 1)
                for b in range(GB):
                    for c in range(C):
                        m = pe.matmul(ps[:, 4, nodes(b)], h_t[:, c, nodes(b)], buf_a[:, c, nodes(b)],
                                      start=(c == 0), stop=(c == C - 1))
                m.then_inc(S("rel_done"), 1)
                turn(g + 1, 5)
                pe.wait_ge(S("rel_ready"), g + 1)
                pe.wait_ge(S("v_ready"), g + 1)
                for b in range(GB):
                    if b == GB // 2:
                        pe.wait_ge(S("rel2_ready"), g + 1)
                        for k in range(GB):
                            m = pe.matmul(ps[:, 7, k:k + 1], rel2[:, nodes(k)], ones[:, 0:1], start=True, stop=True)
                        m.then_inc(S("nrm_done"), 1)
                    m = pe.matmul(half_bank(2, b), rel[:, nodes(b)], vals[:, 0, b, :], start=True, stop=True)
                m.then_inc(S("out0_done"), 1)

            l0(0, True)
            pe.wait_ge(S("nrm_ready"), 1)
            pe.wait_ge(su_dve, 2)
            pe.transpose(ps[:, 7, 0:N], adj_s[:], ident[:])
            for c in range(C):
                m = pe.matmul(ps[:, 7, D:2 * D], bv_rep[:, c, :], w_o[:, c, :], start=(c == 0), stop=(c == C - 1))
            m.then_inc(su_pe, 1)
            pe.wait_ge(su_dve, 3)
            with pe.Fori(1, G) as g:
                l0(g, False)

            def qk(g, first):
                if not first:
                    pe.wait_ge(S("masked"), 4 * g)
                pe.wait_ge(hi_ready, g + G + 1)
                proj_t(0, q1_hi, q1_lo, "hi")
                pe.wait_ge(lo_ready, g + G + 1)
                proj_t(0, q1_hi, q1_lo, "lo").then_inc(S("q_done"), 1)

            def k(g):
                for f in range(C):
                    cols = slice(f * P, (f + 1) * P)
                    for i, (w, h) in enumerate(((k1_hi, h_hi), (k1_lo, h_hi), (k1_hi, h_lo))):
                        for c in range(C):
                            m = pe.matmul(ps[:, 2 + f, :], w[:, c, cols], h[:, c, :], start=(i == 0 and c == 0),
                                          stop=(i == 2 and c == C - 1), skip_group_check=True)
                    m.then_inc(S("k_done"), 1)

            def scores(g, half):
                if not half:
                    pe.wait_ge(S("q_ready"), g + 1)
                    pe.wait_ge(S("k_ready"), C * g + 1)
                for b2 in range(PB):
                    for f in range(C):
                        for r in range(R):
                            if not half and b2 == 0 and f == 0 and r == 2 + C - 1:
                                pe.wait_ge(S("k_ready"), C * g + 2)
                            hd = slice(r * HD, (r + 1) * HD)
                            o = b2 * C * N + f * N
                            m = pe.matmul(ps[:, r, o:o + N], buf_a[hd, f, nodes(PB * half + b2)],
                                          buf_b[hd, f, nodes(PB * half + b2)], start=True, stop=True)
                m.then_inc(S("s_done"), 1)

            def attend(half, p, project):
                def turn_p(j):
                    b2, f = divmod(j, C)
                    pe.wait_ge(S("prob_ready"), 2 * p + b2 + 1)
                    if j >= 2:
                        pe.wait_ge(S("pt_ready"), 4 * p + j - 1)
                    for r in range(R):
                        m = pe.transpose(ps[:, 4 + f, nodes(r)], pr[:, half, b2, r, f, :], ident[:])
                    m.then_inc(S("pt_done"), 1)

                def apply_p(j):
                    b2, f = divmod(j, C)
                    pe.wait_ge(S("pt_ready"), 4 * p + j + 1)
                    if j == 0 and not (isinstance(p, int) and p == 0):
                        pe.wait_ge(S("o_lo_ready"), p)
                    o = f * PB * N + b2 * N
                    for r in range(R):
                        v_cols = slice(f * P + r * HD, f * P + (r + 1) * HD)
                        m = pe.matmul(ps[r * HD:(r + 1) * HD, 6, o:o + N], vals[:, 0, 2 * half + b2, v_cols],
                                      pr_t[:, j % 2, r, :], start=True, stop=True)
                    return m

                turn_p(0)
                turn_p(1)
                if project:
                    project_o(p - 1, 0)
                apply_p(0)
                turn_p(2)
                apply_p(1)
                turn_p(3)
                if project:
                    project_o(p - 1, 1)
                apply_p(2)
                apply_p(3).then_inc(S("pv_done"), 1)

            def project_o(p, b2):
                if b2 == 0:
                    pe.wait_ge(S("o_lo_ready"), p + 1)
                    if not (isinstance(p, int) and p == 0):
                        pe.wait_ge(S("fin1"), p)
                m = proj_n(half_bank(7, b2), (o_hi, o_lo), nodes(b2), o1_hi, o1_lo)
                if b2 == PB - 1:
                    m.then_inc(S("y_done"), 1)

            def l1(g, first):
                qk(g, first)
                k(g)
                scores(g, 0)
                if not first:
                    attend(1, 2 * g - 1, True)
                pe.wait_ge(S("masked"), 4 * g + 2)
                turn(g + G + 1, 0)
                for b in range(GB):
                    m = proj_n(half_bank(4, b), (h_hi, h_lo), nodes(b), v1_hi, v1_lo)
                m.then_inc(S("v1_done"), 1)
                pe.wait_ge(ht_ready, g + G + 2)
                scores(g, 1)
                pe.wait_ge(S("v1_ready"), g + 1)
                attend(0, 2 * g, not first)

            pe.wait_ge(S("fin0"), G)
            pe.wait_ge(su_lo, 1)
            l1(0, True)
            with pe.Fori(1, G) as g:
                l1(g, False)
            attend(1, NP - 1, True)
            for b2 in range(PB):
                project_o(NP - 1, b2)

            def sum_rows(g, first):
                pe.wait_ge(hi_ready, g + 2 * G + 1)
                if not first:
                    pe.wait_ge(S("e_ready"), g)
                for w in (s2_hi, s2_lo):
                    for c in range(C):
                        pe.matmul(ps[:, 4, :], w[:, c, :], h_hi[:, c, :], start=(w is s2_hi and c == 0), stop=False,
                                  skip_group_check=True)
                pe.wait_ge(lo_ready, g + 2 * G + 1)
                for c in range(C):
                    m = pe.matmul(ps[:, 4, :], s2_hi[:, c, :], h_lo[:, c, :], start=False, stop=(c == C - 1),
                                  skip_group_check=True)
                m.then_inc(S("s2_done"), 1)

            def project2(g, first):
                if not first:
                    pe.wait_ge(S("h_ready"), g)
                for b in (2, 3, 0, 1):
                    if b == 0 and not (isinstance(g, int) and g < 2):
                        pe.wait_ge(S("ry_ready"), g - 1)
                    m = proj_n(ps[:, b, 0:D + 2], (h_hi, h_lo), nodes(b), w2_hi, w2_lo)
                m.then_inc(S("h_done"), 1)

            def turn_p2(g):
                pe.wait_ge(S("p2_ready"), g)
                for b in range(GB):
                    m = pe.transpose(ps[:, 7, nodes(b)], p2[:, b, :], ident[:])
                m.then_inc(S("p2_turned"), 1)

            def attend2(g, slot, last):
                pe.wait_ge(S("p2t_ready"), g)
                pe.wait_ge(S("h_ready"), g if last else g + 1)
                for b in range(GB):
                    m = pe.matmul(half_bank(0, b), p2_t[:, b, :], vals[:, slot, b, :], start=True, stop=True)
                m.then_inc(S("att_done"), 1)

            def l2(g, slot, first, last):
                sum_rows(g, first)
                project2(g, first)
                if not first:
                    turn_p2(g)
                if not last:
                    turn(g + 2 * G + 1, 5)
                if not first:
                    attend2(g, 1 - slot, False)

            pe.wait_ge(S("fin1"), NP)
            l2(0, 0, True, False)
            l2(1, 1, False, False)
            with pe.Fori(0, (G - 4) // 2) as i:
                l2(2 * i + 2, 0, False, False)
                l2(2 * i + 3, 1, False, False)
            l2(G - 2, 0, False, False)
            l2(G - 1, 1, False, True)
            turn_p2(G)
            attend2(G, 1, True)

            def gather(g):
                pe.wait_ge(S("hn_ready"), g + 1)
                if not (isinstance(g, int) and g == 0):
                    pe.wait_ge(S("a_lo_ready"), g)
                for b in range(GB):
                    for c in range(C):
                        m = pe.matmul(ps[:, c, nodes(b)],
                                      buf_a[:].rearrange("p c (b d) -> p (c b) d", d=D)[:, b, c * P:(c + 1) * P],
                                      norm_adj_t[:], start=True, stop=True)
                m.then_inc(S("a_done"), 1)

            def project3(g, slot):
                pe.wait_ge(S("a_lo_ready"), g + 1)
                if not (isinstance(g, int) and g == 0):
                    pe.wait_ge(S("fin3"), g)
                for b in range(GB):
                    m = proj_n(half_bank(2, b), (a_hi[:, slot], a_lo[slot]), nodes(b), w3_hi, w3_lo)
                m.then_inc(S("out3_done"), 1)

            pe.wait_ge(S("ry_ready"), G)
            gather(0)
            gather(1)
            project3(0, 0)
            with pe.Fori(0, (G - 2) // 2) as i:
                for k in range(2):
                    gather(2 * i + k + 2)
                    project3(2 * i + k + 1, 1 - k)
            project3(G - 1, 1)

        @block.vector
        def _(dve):
            def stats(n, g, ready, count):
                dve.wait_ge(ready, count)
                for b in range(GB):
                    i = dve.bn_stats(st[:, b, :], xg(g, b, 1))
                i.then_inc(bn_done, 1)
                if not (isinstance(n, int) and n == 0):
                    dve.wait_ge(nmr_ready, n)
                dve.wait_ge(bn_done, n + 1)
                dve.tensor_copy(st_seen[:], st[:, 0, 0:1])
                for b in range(GB):
                    i = dve.bn_aggr(mv[:, b, :], st[:, b, :])
                i.then_inc(S("mv_own"), 1)
                dve.wait_ge(S("mv_own"), n + 1)
                dve.tensor_scalar(neg_mean[:], mv[:, :, 0], -1.0, None, ALU.mult).then_inc(stat_ready, 1)

            def hi_part(n):
                dve.wait_ge(ht_ready, n + 1)
                dve.tensor_copy(h_hi[:], h_t[:]).then_inc(hi_ready, 1)

            def lo_part(n):
                dve.wait_ge(hi_ready, n + 1)
                dve.tensor_tensor(h_lo[:], h_t[:], f32(h_hi[:]), ALU.subtract).then_inc(lo_ready, 1)

            own = [0]

            def mine(i):
                own[0] += 1
                i.then_inc(S("su_own"), 1)
                dve.wait_ge(S("su_own"), own[0])

            def split(hi, lo, src):
                mine(dve.tensor_copy(hi, src))
                return dve.tensor_tensor(lo, src, f32(hi), ALU.subtract)

            stats(0, 0, x_in, 16)
            dve.wait_ge(w_in, 16 * len(loads))
            dve.tensor_reduce(deg[:], adj_n[:], AX_X, ALU.add).then_inc(S("deg_ready"), 1)
            dve.wait_ge(su_pe, 1)
            split(m_hi[:], m_lo[:], ps[:, 0:2, 0:D])
            split(v0_hi[:], v0_lo[:], ps[:, 2:4, 0:D]).then_inc(su_dve, 1)
            hi_part(0)
            lo_part(0)
            stats(1, 1, x_in, 32)
            dve.wait_ge(w_in2, 16 * len(loads2))
            dve.wait_ge(su_pool, 1)
            dve.tensor_scalar(maskb[:], adj_n[:], -1.0, BIG, ALU.add, ALU.mult)
            dve.tensor_scalar(beta_i[:], ident[:], beta_c[:, 0:1], None, ALU.mult)
            mine(dve.tensor_scalar(b3_row[:], b3_row[:], -1.0, None, ALU.add))
            dve.tensor_scalar(bqs_c[:], bq_c[:], float(HD) ** -0.5, None, ALU.mult)
            for c in range(C):
                dve.tensor_scalar(bv_rep[:, c, :], ones[:], bv_c[:, c:c + 1], None, ALU.mult)
            dve.wait_ge(S("dis_ready"), 1)
            mine(dve.tensor_scalar(deg_pos[:], deg[:], 0.0, None, ALU.is_gt))
            mine(dve.tensor_tensor(dis[:], deg_pow[:], deg_pos[:], ALU.mult))
            dve.tensor_scalar(adj_s[:], adj_n[:], dis[:, 0:1], None, ALU.mult).then_inc(su_dve, 1)

            def l0(g, stats_args):
                if stats_args:
                    stats(g + 2, *stats_args)
                dve.wait_ge(S("rel_done"), g + 1)
                dve.tensor_tensor(rel[:].rearrange("p (b n) -> p b n", b=GB),
                                  ps[:, 4, :].rearrange("p (b n) -> p b n", b=GB),
                                  bc(adj_n[:], GB), ALU.mult).then_inc(S("rel_ready"), 1)
                hi_part(g + 1)
                dve.wait_ge(S("nrm_done"), g + 1)
                dve.tensor_copy(nrm[:], ps[:, 7, 0:GB]).then_inc(S("nrm_ready"), 1)
                lo_part(g + 1)
                dve.wait_ge(S("out0_done"), g + 1)
                dve.wait_ge(S("rnrm_ready"), g + 1)
                for b in range(GB):
                    i = dve.scalar_tensor_tensor(xg(g, b, 1), ps[:, 2 + b // 2, (b % 2) * D:(b % 2 + 1) * D],
                                                 rnrm[:, b:b + 1], xg(g, b, 1), ALU.mult, ALU.add)
                i.then_inc(S("fin0"), 1)

            l0(0, (2, x_in, 48))
            dve.wait_ge(su_pe, 2)
            dve.tensor_scalar(norm_adj_t[:], ps[:, 7, 0:N], dis[:, 0:1], None, ALU.mult)
            dve.tensor_tensor(bo_row[:], ps[:, 7, D:2 * D], bo_row[:], ALU.add).then_inc(su_dve, 1)
            for c in range(C):
                for t in range(2):
                    mine(dve.tensor_tensor(w2junk[:], w2x[:, c, 0:D], a_row[:, t, :], ALU.mult))
                    mine(dve.tensor_reduce(w2c[:, c, t:t + 1], w2junk[:], AX_X, ALU.add))
            for c in range(C):
                dve.tensor_copy(w2x[:, c, D:D + 2], w2c[:, c, 0:1].broadcast_to([P, 2]))
                mine(dve.tensor_scalar(w2rep[:, c, :], ones[:], w2c[:, c, 1:2], None, ALU.mult))
            split(w2_hi[:], w2_lo[:], w2x[:])
            split(s2_hi[:], s2_lo[:], w2rep[:])
            with dve.Fori(1, G - 2) as g:
                l0(g, (g + 2, x_in, g * 16 + 48))
            l0(G - 2, (0, S("fin0"), 1))
            l0(G - 1, (1, S("fin0"), 2))

            def mask_max(g, half):
                p = 2 * g + half
                dve.wait_ge(S("s_done"), p + 1)
                for b2 in range(PB):
                    if not (isinstance(g, int) and p < 1):
                        dve.wait_ge(S("shifted"), 2 * p + b2 - 1)
                    dve.tensor_tensor(sc[:, b2], ps[:, 0:R, b2 * C * N:(b2 + 1) * C * N].rearrange(
                        "p r (f n) -> p r f n", f=C),
                        maskb[:].unsqueeze(1).unsqueeze(1).broadcast_to([P, R, C, N]), ALU.add)\
                       .then_inc(S("masked"), 1)
                    dve.wait_ge(S("masked"), 2 * p + b2 + 1)
                    dve.tensor_reduce(mx[:, b2, :], sc[:, b2].rearrange("p r f n -> p (r f) n"), AX_X,
                                      ALU.max).then_inc(S("max_ready"), 1)

            def sum_probs(p, half, b2):
                dve.wait_ge(S("exp_ready"), 2 * p + b2 + 1)
                dve.tensor_reduce(sums[:, b2], pr[:, half, b2].rearrange("p r f n -> p (r f) n"), AX_X, ALU.add)\
                   .then_inc(S("sums_own"), 1)
                dve.wait_ge(S("sums_own"), 2 * p + b2 + 1)
                if not (isinstance(p, int) and p == 0):
                    dve.wait_ge(S("prob_ready"), 2 * p + b2 - 1)
                dve.reciprocal(rinv[:, b2], sums[:, b2]).then_inc(S("rinv_ready"), 1)

            def o_lo_part(p):
                dve.wait_ge(S("o_hi_ready"), p + 1)
                dve.tensor_tensor(flat(o_lo[:]), ps[:, 6, :], f32(flat(o_hi[:])), ALU.subtract)\
                   .then_inc(S("o_lo_ready"), 1)

            def add1(g, half, p):
                dve.wait_ge(S("y_done"), p + 1)
                dve.wait_ge(S("bias1"), g + 1)
                dve.tensor_tensor(xg(g, PB * half, PB), ps[:, 7, :], xg(g, PB * half, PB), ALU.add)\
                   .then_inc(S("fin1"), 1)

            def l1(g, first, stats_args):
                mask_max(g, 0)
                if not first:
                    add1(g - 1, 0, 2 * g - 2)
                sum_probs(2 * g, 0, 0)
                if not first:
                    o_lo_part(2 * g - 1)
                sum_probs(2 * g, 0, 1)
                stats(g + G + 2, *stats_args)
                mask_max(g, 1)
                if not first:
                    add1(g - 1, 1, 2 * g - 1)
                sum_probs(2 * g + 1, 1, 0)
                o_lo_part(2 * g)
                sum_probs(2 * g + 1, 1, 1)

            l1(0, True, (2, S("fin0"), G))
            with dve.Fori(1, G - 2) as g:
                l1(g, False, (g + 2, S("fin0"), G))
            l1(G - 2, False, (0, S("fin1"), 2))
            l1(G - 1, False, (1, S("fin1"), 4))
            add1(G - 1, 0, NP - 2)
            o_lo_part(NP - 1)
            add1(G - 1, 1, NP - 1)

            def l2(g, first, last, stats_args):
                if not first:
                    dve.wait_ge(S("p2_turned"), g)
                    dve.tensor_tensor(p2_t[:], ps[:, 7, :].rearrange("p (b n) -> p b n", b=GB), bc(beta_i[:], GB),
                                      ALU.add).then_inc(S("p2t_ready"), 1)
                dve.wait_ge(S("s2_done"), g + 1)
                dve.wait_ge(S("s1_ready"), g + 1)
                if not first:
                    dve.wait_ge(S("shifted2"), g)
                dve.tensor_tensor(e2[:], ps[:, 4, :].rearrange("p (b n) -> p b n", b=GB), bcol(s1[:], N),
                                  ALU.add).then_inc(S("e_ready"), 1)
                dve.wait_ge(S("e_ready"), g + 1)
                dve.scalar_tensor_tensor(e2[:], e2[:], ALPHA, e2[:], ALU.mult, ALU.max).then_inc(S("lr_ready"), 1)
                stats(g + 2 * G + 2, *stats_args)
                dve.wait_ge(S("masked2"), g + 1)
                dve.tensor_reduce(mx2[:], e2[:], AX_X, ALU.max).then_inc(S("max2_ready"), 1)
                if not last:
                    lo_part(g + 2 * G + 1)
                if not first:
                    elu_part(g)
                dve.wait_ge(S("exp2_ready"), g + 1)
                dve.tensor_reduce(sum2[:], p2[:], AX_X, ALU.add).then_inc(S("sum2_own"), 1)
                dve.wait_ge(S("sum2_own"), g + 1)
                dve.reciprocal(ri2[:], sum2[:]).then_inc(S("ri2_ready"), 1)

            def elu_part(g):
                dve.wait_ge(S("ry_ready"), g)
                dve.scalar_tensor_tensor(flat(buf_b[:]), flat(buf_b[:]), 1.0, flat(buf_a[:]), ALU.min, ALU.add)\
                   .then_inc(S("elu_ready"), 1)

            l2(0, True, False, (2, S("fin1"), NP))
            with dve.Fori(1, G - 2) as g:
                l2(g, False, False, (g + 2, S("fin1"), NP))
            l2(G - 2, False, False, (0, S("fin2"), 1))
            l2(G - 1, False, True, (1, S("fin2"), 2))
            dve.wait_ge(S("p2_turned"), G)
            dve.tensor_tensor(p2_t[:], ps[:, 7, :].rearrange("p (b n) -> p b n", b=GB), bc(beta_i[:], GB),
                              ALU.add).then_inc(S("p2t_ready"), 1)
            elu_part(G)

            def lo3(g, slot):
                dve.wait_ge(S("a_hi_ready"), g + 1)
                dve.tensor_tensor(a_lo[slot][:], ps[:, 0:2, :], f32(a_hi[:, slot]), ALU.subtract)\
                   .then_inc(S("a_lo_ready"), 1)

            def add3(g):
                dve.wait_ge(S("out3_done"), g + 1)
                dve.wait_ge(S("bias3"), g + 1)
                dve.tensor_tensor(xg(g), flat(ps[:, 2:4, :]), xg(g), ALU.add).then_inc(S("fin3"), 1)

            lo3(0, 0)
            with dve.Fori(0, (G - 2) // 2) as i:
                for k in range(2):
                    stats(2 * i + k + 2 + 3 * G, 2 * i + k + 2, S("fin2"), G)
                    lo3(2 * i + k + 1, 1 - k)
                    add3(2 * i + k)
            lo3(G - 1, 1)
            add3(G - 2)
            add3(G - 1)

        @block.scalar
        def _(act):
            def normalise(n, g):
                act.wait_ge(nmr_ready, n + 1)
                if not (isinstance(n, int) and n == 0):
                    act.wait_ge(turned, n)
                for b in range(GB):
                    i = act.activation(xn[:, b, :], xg(g, b, 1), ACT.Identity, bias=nmr[:, b:b + 1],
                                       scale=rstd[:, b:b + 1])
                i.then_inc(xn_ready, 1)

            def h_part(n, bank):
                act.wait_ge(turned, n + 1)
                act.activation(h_t[:], ps[:, bank:bank + 2, :], ACT.Relu).then_inc(ht_ready, 1)

            def hi_part(n):
                act.wait_ge(ht_ready, n + 1)
                act.activation(h_hi[:], h_t[:], ACT.Copy).then_inc(hi_ready, 1)

            normalise(0, 0)
            h_part(0, 5)

            def l0(g, nxt):
                normalise(g + 1, nxt)
                act.wait_ge(S("g_done"), g + 1)
                act.activation(buf_a[:], ps[:, 0:2, :], ACT.Copy).then_inc(S("gt_ready"), 1)
                act.wait_ge(S("v_done"), g + 1)
                act.activation(flat(vals[:, 0]), flat(ps[:, 2:4, :]), ACT.Copy).then_inc(S("v_ready"), 1)
                act.wait_ge(S("rel_ready"), g + 1)
                act.activation(rel2[:], rel[:], ACT.Square).then_inc(S("rel2_ready"), 1)
                h_part(g + 1, 5)

            l0(0, 1)
            act.wait_ge(w_in2, 16 * len(loads2))
            for i, (hi, lo) in enumerate(staged):
                act.activation(flat(hi[:]), wstage[:, i], ACT.Copy)
            act.activation(o1_hi[:], w_o[:], ACT.Copy).then_inc(su_hi, 1)
            with act.Fori(1, G - 1) as g:
                l0(g, g + 1)
            l0(G - 1, 0)

            def take_turned(p, j):
                act.wait_ge(S("pt_done"), 4 * p + j + 1)
                act.activation(flat(pr_t[:, j % 2]), ps[:, 4 + j % C, :], ACT.Copy).then_inc(S("pt_ready"), 1)

            def exponent(p, half, b2):
                act.wait_ge(S("shifted"), 2 * p + b2 + 1)
                t = pr[:, half, b2].rearrange("p r f n -> p (r f n)")
                act.activation(t, t, ACT.Exp).then_inc(S("exp_ready"), 1)

            def o_hi_part(p):
                act.wait_ge(S("pv_done"), p + 1)
                if not (isinstance(p, int) and p == 0):
                    act.wait_ge(S("y_done"), p)
                act.activation(flat(o_hi[:]), ps[:, 6, :], ACT.Copy).then_inc(S("o_hi_ready"), 1)

            def l1(g, first, nxt):
                act.wait_ge(S("q_done"), g + 1)
                for f in range(C):
                    i = act.activation(buf_a[:, f, :], ps[:, f, :], ACT.Identity, bias=bqs_c[:, f:f + 1],
                                       scale=float(HD) ** -0.5)
                i.then_inc(S("q_ready"), 1)
                for f in range(C):
                    act.wait_ge(S("k_done"), C * g + f + 1)
                    act.activation(buf_b[:, f, :], ps[:, 2 + f, :], ACT.Identity, bias=bk_c[:, f:f + 1])\
                       .then_inc(S("k_ready"), 1)
                normalise(g + G + 1, nxt)
                if not first:
                    for j in range(PB * C):
                        take_turned(2 * g - 1, j)
                exponent(2 * g, 0, 0)
                if not first:
                    o_hi_part(2 * g - 1)
                h_part(g + G + 1, 0)
                exponent(2 * g, 0, 1)
                act.wait_ge(S("v1_done"), g + 1)
                act.activation(flat(vals[:, 0]), flat(ps[:, 4:6, :]), ACT.Copy).then_inc(S("v1_ready"), 1)
                hi_part(g + G + 1)
                for j in range(PB * C):
                    take_turned(2 * g, j)
                exponent(2 * g + 1, 1, 0)
                o_hi_part(2 * g)
                exponent(2 * g + 1, 1, 1)

            act.wait_ge(su_dve, 2)
            l1(0, True, 1)
            with act.Fori(1, G - 1) as g:
                l1(g, False, g + 1)
            l1(G - 1, False, 0)
            for j in range(PB * C):
                take_turned(NP - 1, j)
            o_hi_part(NP - 1)

            def natural(g, first):
                act.wait_ge(nmr_ready, g + 3 * G + 1)
                if not first:
                    act.wait_ge(S("a_done"), g)
                for b in range(GB):
                    i = act.activation(buf_a[:].rearrange("p c (b d) -> p (c b) d", d=D)[:, b, :], xg(g, b, 1),
                                       ACT.Relu, bias=nmr[:, b:b + 1], scale=rstd[:, b:b + 1])
                i.then_inc(S("hn_ready"), 1)

            def output2(g, first):
                act.wait_ge(S("att_done"), g)
                if not first:
                    act.wait_ge(S("fin2"), g - 1)
                act.activation(buf_b[:], ps[:, 0:2, :], ACT.Exp).then_inc(S("ey_done"), 1)
                act.activation(buf_a[:], ps[:, 0:2, :], ACT.Relu).then_inc(S("ry_ready"), 1)

            def l2(g, slot, first, last, nxt):
                if not last:
                    normalise(g + 2 * G + 1, nxt)
                act.wait_ge(S("h_done"), g + 1)
                if not first:
                    act.wait_ge(S("e_ready"), g)
                act.activation(s1[:], ps[:, 0:GB, D], ACT.Copy).then_inc(S("s1_ready"), 1)
                act.activation(vals[:, slot], ps[:, 0:GB, 0:D], ACT.Copy).then_inc(S("h_ready"), 1)
                if not last:
                    h_part(g + 2 * G + 1, 5)
                    hi_part(g + 2 * G + 1)
                if not first:
                    output2(g, isinstance(g, int) and g == 1)
                act.wait_ge(S("shifted2"), g + 1)
                act.activation(p2[:], p2[:], ACT.Exp).then_inc(S("exp2_ready"), 1)

            act.wait_ge(S("fin1"), NP)
            l2(0, 0, True, False, 1)
            l2(1, 1, False, False, 2)
            with act.Fori(0, (G - 4) // 2) as i:
                l2(2 * i + 2, 0, False, False, 2 * i + 3)
                l2(2 * i + 3, 1, False, False, 2 * i + 4)
            l2(G - 2, 0, False, False, G - 1)
            l2(G - 1, 1, False, True, 0)
            output2(G, False)
            act.wait_ge(S("elu_ready"), G)
            natural(0, True)

            def hi3(g, slot):
                act.wait_ge(S("a_done"), g + 1)
                act.activation(a_hi[:, slot], ps[:, 0:2, :], ACT.Copy).then_inc(S("a_hi_ready"), 1)

            hi3(0, 0)
            natural(1, False)
            with act.Fori(0, (G - 2) // 2) as i:
                for k in range(2):
                    hi3(2 * i + k + 1, 1 - k)
                    natural(2 * i + k + 2, False)
            hi3(G - 1, 1)

        @block.gpsimd
        def _(pool):
            def rstd_part(n, last_used, count):
                pool.wait_ge(stat_ready, n + 1)
                pool.tensor_tensor(veps[:], mv[:, :, 1], eps_c[:], ALU.add).then_inc(veps_done, 1)
                if last_used is not None:
                    pool.wait_ge(last_used, count)
                pool.wait_ge(veps_done, n + 1)
                pool.tensor_tensor(rstd[:], veps[:], expo[:], ALU.pow).then_inc(rstd_done, 1)
                pool.wait_ge(rstd_done, n + 1)
                pool.tensor_tensor(nmr[:], neg_mean[:], rstd[:], ALU.mult).then_inc(nmr_ready, 1)

            def lo_part(n):
                pool.wait_ge(hi_ready, n + 1)
                pool.tensor_tensor(h_lo[:], h_t[:], f32(h_hi[:]), ALU.subtract).then_inc(lo_ready, 1)

            def add_row(g, row, name):
                v = xg(g).rearrange("p (b d) -> p b d", b=GB)
                pool.tensor_tensor(v, v, row[:].unsqueeze(1).broadcast_to([P, GB, D]), ALU.add).then_inc(S(name), 1)

            pool.memset(expo[:], -0.5)
            pool.memset(eps_c[:], EPS)
            pool.memset(ones[:], 1.0)
            pool.memset(ident[:], 0.0).then_inc(S("su_zero"), 1)
            pool.wait_ge(S("su_zero"), 1)
            pool.affine_select(out=ident[:], in_=ident[:], compare_op=ALU.not_equal, fill=1.0, base=0,
                               pattern=[[-1, P]], channel_multiplier=1).then_inc(su_pool, 1)
            pool.wait_ge(su_pool, 1)
            rstd_part(0, None, 0)
            pool.wait_ge(S("deg_ready"), 1)
            pool.tensor_scalar(deg_safe[:], deg[:], TINY, None, ALU.max).then_inc(S("dis_own"), 1)
            rstd_part(1, xn_ready, 1)
            pool.wait_ge(S("dis_own"), 1)
            pool.tensor_tensor(deg_pow[:], deg_safe[:], expo[:, 0:1], ALU.pow).then_inc(S("dis_ready"), 1)

            def l0(g):
                rstd_part(g + 2, xn_ready, g + 2)
                pool.wait_ge(S("nrm_ready"), g + 1)
                pool.tensor_tensor(rnrm[:], nrm[:], expo[:], ALU.pow).then_inc(S("rnrm_ready"), 1)

            l0(0)
            pool.wait_ge(su_hi, 1)
            for i, (hi, lo) in enumerate(staged):
                pool.tensor_tensor(flat(lo[:]), wstage[:, i], f32(flat(hi[:])), ALU.subtract)
            pool.tensor_tensor(o1_lo[:], w_o[:], f32(o1_hi[:]), ALU.subtract).then_inc(su_lo, 1)
            with pool.Fori(1, G) as g:
                l0(g)

            def shift_scores(g, half, b2):
                p = 2 * g + half
                pool.wait_ge(S("max_ready"), 2 * p + b2 + 1)
                if not (isinstance(g, int) and p < 2):
                    pool.wait_ge(S("pt_done"), 4 * p - 4)
                pool.tensor_tensor(pr[:, half, b2].rearrange("p r f n -> p (r f) n"),
                                   sc[:, b2].rearrange("p r f n -> p (r f) n"), bcol(mx[:, b2, :], N),
                                   ALU.subtract).then_inc(S("shifted"), 1)

            def scale_probs(p, half, b2):
                pool.wait_ge(S("rinv_ready"), 2 * p + b2 + 1)
                t = pr[:, half, b2].rearrange("p r f n -> p (r f) n")
                pool.tensor_tensor(t, t, bcol(rinv[:, b2, :], N), ALU.mult).then_inc(S("prob_ready"), 1)

            def l1(g):
                for half in range(2):
                    for b2 in range(PB):
                        shift_scores(g, half, b2)
                    if half:
                        rstd_part(g + G + 2, xn_ready, g + G + 2)
                    for b2 in range(PB):
                        scale_probs(2 * g + half, half, b2)
                    if not half:
                        lo_part(g + G + 1)
                pool.wait_ge(S("fin0"), g + 1)
                add_row(g, bo_row, "bias1")

            pool.wait_ge(su_dve, 3)
            l1(0)
            with pool.Fori(1, G) as g:
                l1(g)

            def add2(g):
                pool.wait_ge(S("elu_ready"), g)
                pool.tensor_tensor(xg(g - 1), flat(buf_b[:]), xg(g - 1), ALU.add).then_inc(S("fin2"), 1)

            def l2(g, first, last):
                pool.wait_ge(S("lr_ready"), g + 1)
                pool.tensor_tensor(e2[:], e2[:], bc(adj_n[:], GB), ALU.mult).then_inc(S("masked2"), 1)
                pool.wait_ge(S("max2_ready"), g + 1)
                if not first:
                    pool.wait_ge(S("p2_turned"), g)
                pool.tensor_tensor(p2[:], e2[:], bcol(mx2[:], N), ALU.subtract).then_inc(S("shifted2"), 1)
                if not last:
                    rstd_part(g + 2 * G + 2, xn_ready, g + 2 * G + 2)
                pool.wait_ge(S("ri2_ready"), g + 1)
                pool.tensor_tensor(p2[:], p2[:], bcol(ri2[:], N), ALU.mult).then_inc(S("p2_ready"), 1)
                if not first:
                    add2(g)

            l2(0, True, False)
            with pool.Fori(1, G - 1) as g:
                l2(g, False, False)
            l2(G - 1, False, True)
            add2(G)

            pool.wait_ge(S("hn_ready"), 1)
            rstd_part(3 * G + 1, S("hn_ready"), 1)
            add_row(0, b3_row, "bias3")
            with pool.Fori(2, G) as g:
                rstd_part(g + 3 * G, S("hn_ready"), g)
                add_row(g - 1, b3_row, "bias3")
            pool.wait_ge(S("hn_ready"), G)
            add_row(G - 1, b3_row, "bias3")


_INS = ['x', 'adj', 'L0_gnn_Wq', 'L0_gnn_Wk', 'L0_gnn_Wv', 'L1_gnn_Wq', 'L1_gnn_bq', 'L1_gnn_Wk', 'L1_gnn_bk',
        'L1_gnn_Wv', 'L1_gnn_bv', 'L1_gnn_Wo', 'L1_gnn_bo', 'L2_gnn_W', 'L2_gnn_a', 'L2_gnn_beta',
        'L3_gnn_weight', 'L3_gnn_bias']
_OUTS = [((64, 128, 256), 'float32')]


def kernel(**inputs):
    import numpy as _np
    import concourse.bacc as _bacc
    from concourse import mybir as _mybir
    from concourse.bass_utils import run_bass_kernel_spmd as _run

    nc = _bacc.Bacc("TRN2", target_bir_lowering=False, num_devices=1)
    arrays, args = {}, []
    for name in _INS:
        a = _np.ascontiguousarray(inputs[name])
        arrays[f"in_{name}_dram"] = a
        args.append(nc.dram_tensor(f"in_{name}_dram", a.shape, _mybir.dt.from_np(a.dtype), kind="ExternalInput").ap())
    for i, (shape, dtype) in enumerate(_OUTS):
        dt = _mybir.dt.from_np(_np.dtype(dtype))
        args.append(nc.dram_tensor(f"out_{i}_dram", shape, dt, kind="ExternalOutput").ap())
    four_layer_graph_kernel(nc, *args)
    r = _run(nc, [arrays], core_ids=[0])
    got = tuple(r.results[0][f"out_{i}_dram"] for i in range(len(_OUTS)))
    return got[0]
```

```python
from contextlib import ExitStack

import concourse.bass as bass
from concourse import mybir

ALU = mybir.AluOpType
ACT = mybir.ActivationFunctionType
F32 = mybir.dt.float32
F32R = mybir.dt.float32r
AX_X = mybir.AxisListType.X


def four_layer_graph_kernel(nc, x, adj, L0_gnn_Wq, L0_gnn_Wk, L0_gnn_Wv,
                            L1_gnn_Wq, L1_gnn_bq, L1_gnn_Wk, L1_gnn_bk, L1_gnn_Wv, L1_gnn_bv,
                            L1_gnn_Wo, L1_gnn_bo, L2_gnn_W, L2_gnn_a, L2_gnn_beta,
                            L3_gnn_weight, L3_gnn_bias, out):
    B, N, D = x.shape
    P = 128
    GB = 4
    G = B // GB
    C = D // P
    GN = GB * N
    GD = GB * D
    H = 8
    HD = D // H
    R = P // HD
    PB = 2
    NP = B // PB
    EPS = 1e-05
    ALPHA = 0.2
    BIG = 1000000000.0
    TINY = 1e-30
    assert N == P and GN == 512 and C == 2 and R == 4

    ctx = ExitStack()
    with ctx:
        def sb(name, shape, dt=F32):
            return ctx.enter_context(nc.sbuf_tensor(name, shape, dt))

        def sem(name):
            return ctx.enter_context(nc.semaphore(name))

        ps = ctx.enter_context(nc.psum_tensor("ps", [P, 8, 512], F32))

        xs = sb("xs", [P, B * D])
        adj_n = sb("adj_n", [P, N])
        ident = sb("ident", [P, P])
        ones = sb("ones", [P, P])
        maskb = sb("maskb", [P, N])
        beta_i = sb("beta_i", [P, N])
        beta_c = sb("beta_c", [P, 1])
        deg = sb("deg", [P, 1])
        deg_pos = sb("deg_pos", [P, 1])
        deg_safe = sb("deg_safe", [P, 1])
        deg_pow = sb("deg_pow", [P, 1])
        dis = sb("dis", [P, 1])
        adj_s = sb("adj_s", [P, N])
        norm_adj_t = sb("norm_adj_t", [P, N])
        expo = sb("expo", [P, GB])
        eps_c = sb("eps_c", [P, GB])
        bo_row = sb("bo_row", [P, D])
        b3_row = sb("b3_row", [P, D])
        bq_c = sb("bq_c", [P, C])
        bqs_c = sb("bqs_c", [P, C])
        bk_c = sb("bk_c", [P, C])
        bv_c = sb("bv_c", [P, C])
        bv_rep = sb("bv_rep", [P, C, P])
        a_row = sb("a_row", [P, 2, D])
        wq0 = sb("wq0", [P, C, D])
        wk0 = sb("wk0", [P, C, D])
        wv0 = sb("wv0", [P, C, D])
        wstage = sb("wstage", [P, 4, C * D])
        w_o = sb("w_o", [P, C, D])
        w2x = sb("w2x", [P, C, D + 2])
        w2c = sb("w2c", [P, C, 2])
        w2junk = sb("w2junk", [P, D])
        w2rep = sb("w2rep", [P, C, P])
        m_hi, m_lo = sb("m_hi", [P, C, D], F32R), sb("m_lo", [P, C, D], F32R)
        v0_hi, v0_lo = sb("v0_hi", [P, C, D], F32R), sb("v0_lo", [P, C, D], F32R)
        q1_hi, q1_lo = sb("q1_hi", [P, C, D], F32R), sb("q1_lo", [P, C, D], F32R)
        k1_hi, k1_lo = sb("k1_hi", [P, C, D], F32R), sb("k1_lo", [P, C, D], F32R)
        v1_hi, v1_lo = sb("v1_hi", [P, C, D], F32R), sb("v1_lo", [P, C, D], F32R)
        o1_hi, o1_lo = sb("o1_hi", [P, C, D], F32R), sb("o1_lo", [P, C, D], F32R)
        w3_hi, w3_lo = sb("w3_hi", [P, C, D], F32R), sb("w3_lo", [P, C, D], F32R)
        w2_hi, w2_lo = sb("w2_hi", [P, C, D + 2], F32R), sb("w2_lo", [P, C, D + 2], F32R)
        s2_hi, s2_lo = sb("s2_hi", [P, C, P], F32R), sb("s2_lo", [P, C, P], F32R)
        st = sb("st", [P, GB, 6])
        st_seen = sb("st_seen", [P, 1])
        mv = sb("mv", [P, GB, 2])
        neg_mean = sb("neg_mean", [P, GB])
        veps = sb("veps", [P, GB])
        rstd = sb("rstd", [P, 2, GB])
        nmr = sb("nmr", [P, 2, GB])
        xn = sb("xn", [P, GB, D])
        h_t = sb("h_t", [P, C, GN])
        h_hi = sb("h_hi", [P, C, GN], F32R)
        h_lo = sb("h_lo", [P, C, GN], F32R)
        buf_a = sb("buf_a", [P, C, GN])
        buf_b = sb("buf_b", [P, C, GN])
        vals = sb("vals", [P, 2, GB, D])
        rel = sb("rel", [P, GN])
        rel2 = sb("rel2", [P, GN])
        nrm = sb("nrm", [P, GB])
        rnrm = sb("rnrm", [P, GB])
        sc = wstage[:].rearrange("p (b r) m -> p (b r m)", b=PB).rearrange(
            "p (b r f n) -> p b r f n", b=PB, r=R, f=C)
        mx = sb("mx", [P, PB, R * C])
        pr = sb("pr", [P, 2, PB, R, C, N])
        sums = sb("sums", [P, PB, R * C])
        rinv = sb("rinv", [P, PB, R * C])
        pr_t = sb("pr_t", [P, 2, R, N])
        o_hi = sb("o_hi", [P, C, PB * N], F32R)
        o_lo = sb("o_lo", [P, C, PB * N], F32R)
        s1 = sb("s1", [P, GB])
        e2 = sb("e2", [P, GB, N])
        p2 = sb("p2", [P, GB, N])
        p2_t = sb("p2_t", [P, GB, N])
        elu1 = [pr[:, 0, k].rearrange("p r f n -> p (r f n)") for k in range(2)]
        mx2 = sb("mx2", [P, GB])
        sum2 = sb("sum2", [P, GB])
        ri2 = sb("ri2", [P, GB])
        hn = [pr[:, 1, k].rearrange("p r f n -> p (r f n)").rearrange("p (b d) -> p b d", b=GB) for k in range(2)]
        a_hi = sb("a_hi", [P, 2, C, GN], F32R)
        a_lo = (h_hi, h_lo)
        v_hi, v_lo = [a_hi[:, k].rearrange("p c n -> p (c n)") for k in range(2)]
        rel_hi, rel_lo = [t[:].rearrange("p c n -> p (c n)") for t in (o_hi, o_lo)]

        A_BANK = (5, 2)

        sems = {}

        def S(name):
            if name not in sems:
                sems[name] = sem(name)
            return sems[name]

        w_in, w_in2, x_in, x_out = S("w_in"), S("w_in2"), S("x_in"), S("x_out")
        su_pool, su_dve, su_pe, su_hi, su_lo = S("su_pool"), S("su_dve"), S("su_pe"), S("su_hi"), S("su_lo")
        bn_done, stat_ready, veps_done = S("bn_done"), S("stat_ready"), S("veps_done")
        rstd_done, nmr_ready = S("rstd_done"), S("nmr_ready")
        xn_ready, turned, ht_ready, hi_ready, lo_ready = S("xn_ready"), S("turned"), S("ht_ready"), S("hi_ready"), S("lo_ready")

        def xg(g, b=0, nb=GB):
            return xs[:, bass.ds(g * GD + b * D, nb * D)]

        def bc(ap, reps):
            return ap.unsqueeze(1).broadcast_to([P, reps, N])

        def bcol(ap, cols):
            return ap.unsqueeze(2).broadcast_to([P, ap.shape[1], cols])

        def flat(ap):
            return ap.rearrange("p a n -> p (a n)")

        def f32(ap):
            return ap.bitcast(F32)

        def rows(w):
            return w.rearrange("(c p) f -> p c f", p=P)

        loads = [(wq0[:], rows(L0_gnn_Wq)), (wk0[:], rows(L0_gnn_Wk)), (wv0[:], rows(L0_gnn_Wv)), (adj_n[:], adj)]
        loads2 = [(t[:], v.rearrange("(c p) -> p c", p=P)) for t, v in
                  ((bq_c, L1_gnn_bq), (bk_c, L1_gnn_bk), (bv_c, L1_gnn_bv))]
        loads2 += [(t[:], v.partition_broadcast(P)) for t, v in
                   ((bo_row, L1_gnn_bo), (b3_row, L3_gnn_bias), (beta_c, L2_gnn_beta))]
        loads2 += [(w_o[:], rows(L1_gnn_Wo))]
        loads2 += [(wstage[:, i].rearrange("p (c f) -> p c f", c=C), rows(w))
                   for i, w in enumerate((L1_gnn_Wq, L1_gnn_Wk, L1_gnn_Wv, L3_gnn_weight))]
        loads2 += [(w2x[:, :, 0:D], rows(L2_gnn_W))]
        loads2 += [(a_row[:], L2_gnn_a.rearrange("(t f) o -> (o t) f", t=2).partition_broadcast(P))]
        staged = [(q1_hi, q1_lo), (k1_hi, k1_lo), (v1_hi, v1_lo), (w3_hi, w3_lo)]

        block = ctx.enter_context(nc.Block())

        @block.sync
        def _(sp):
            def load_x(g):
                sp.dma_start(xg(g).rearrange("p (b d) -> p b d", b=GB),
                             x[bass.ds(g * GB, GB)].rearrange("b n d -> n b d")).then_inc(x_in, 16)

            load_x(0)
            with nc.allow_non_contiguous_dma(reason="bias columns"):
                for dst, src in loads:
                    sp.dma_start(dst, src).then_inc(w_in, 16)
                sp.wait_ge(x_in, 16)
                load_x(1)
                for dst, src in loads2:
                    sp.dma_start(dst, src).then_inc(w_in2, 16)
            with sp.Fori(2, G) as g:
                sp.wait_ge(x_in, g * 16)
                load_x(g)
            with sp.Fori(0, G - 1) as g:
                sp.wait_ge(S("fin3"), g + 1)
                sp.dma_start(out[bass.ds(g * GB, GB)].rearrange("b n d -> n b d"),
                             xg(g).rearrange("p (b d) -> p b d", b=GB)).then_inc(x_out, 16)
            for i in range(2):
                sp.wait_ge(S("fin3"), G + i)
                sp.dma_start(out[bass.ds((G - 1) * GB + PB * i, PB)].rearrange("b n d -> n b d"),
                             xg(G - 1, PB * i, PB).rearrange("p (b d) -> p b d", b=PB)).then_inc(x_out, 16)
            sp.wait_ge(x_out, 16 * (G + 1))

        @block.tensor
        def _(pe):
            def proj_t(bank, w_hi, w_lo, part):
                h = h_hi if part == "hi" else h_lo
                for f in range(C):
                    for w in ((w_hi, w_lo) if part == "hi" else (w_hi,)):
                        for c in range(C):
                            m = pe.matmul(ps[:, bank + f, :], w[:, c, f * P:(f + 1) * P], h[:, c, :],
                                          start=(part == "hi" and w is w_hi and c == 0),
                                          stop=(part == "lo" and c == C - 1), skip_group_check=True)
                return m

            def proj_n(o, hs, cols, w_hi, w_lo):
                for i, (h, w) in enumerate(((hs[0], w_hi), (hs[0], w_lo), (hs[1], w_hi))):
                    for c in range(C):
                        m = pe.matmul(o, h[:, c, cols], w[:, c, :], start=(i == 0 and c == 0),
                                      stop=(i == 2 and c == C - 1), skip_group_check=True)
                return m

            def nodes(b):
                return slice(b * N, (b + 1) * N)

            def half_bank(bank, b):
                return ps[:, bank + b // 2, (b % 2) * D:(b % 2 + 1) * D]

            def turn(n, bank):
                pe.wait_ge(xn_ready, n + 1)
                for c in range(C):
                    for b in range(GB):
                        m = pe.transpose(ps[:, bank + c, nodes(b)], xn[:, b, c * P:(c + 1) * P], ident[:])
                m.then_inc(turned, 1)

            pe.wait_ge(su_pool, 1)
            pe.wait_ge(w_in, 16 * len(loads))
            for dc in range(C):
                for ec in range(C):
                    m = pe.matmul(ps[:, dc, 0:D], wq0[:, ec, dc * P:(dc + 1) * P], wk0[:, ec, :],
                                  start=(ec == 0), stop=(ec == C - 1))
            for dc in range(C):
                for ec in range(C):
                    m = pe.transpose(ps[:, 2 + dc, ec * P:(ec + 1) * P], wv0[:, ec, dc * P:(dc + 1) * P], ident[:])
            m.then_inc(su_pe, 1)
            turn(0, 5)
            pe.wait_ge(su_dve, 1)

            def l0(g, first):
                pe.wait_ge(hi_ready, g + 1)
                proj_t(0, m_hi, m_lo, "hi")
                pe.wait_ge(lo_ready, g + 1)
                proj_t(0, m_hi, m_lo, "lo").then_inc(S("g_done"), 1)
                if first:
                    pe.wait_ge(su_dve, 2)
                else:
                    pe.wait_ge(S("fin0"), g)
                v0(0)
                pe.wait_ge(S("gt_ready"), g + 1)
                for b in range(GB):
                    for c in range(C):
                        m = pe.matmul(ps[:, 4, nodes(b)], h_t[:, c, nodes(b)], buf_a[:, c, nodes(b)],
                                      start=(c == 0), stop=(c == C - 1))
                m.then_inc(S("rel_done"), 1)
                v0(1)
                turn(g + 1, 5)
                pe.wait_ge(S("rel_lo_ready"), g + 1)
                pe.wait_ge(S("v_lo_ready"), 2 * g + 1)
                apply_rel(0)
                pe.wait_ge(S("rel2_ready"), g + 1)
                for k in range(GB):
                    m = pe.matmul(ps[:, 7, k:k + 1], rel2[:, nodes(k)], ones[:, 0:1], start=True, stop=True)
                m.then_inc(S("nrm_done"), 1)
                pe.wait_ge(S("v_lo_ready"), 2 * g + 2)
                apply_rel(1).then_inc(S("out0_done"), 1)

            def v0(half):
                for b in (2 * half, 2 * half + 1):
                    m = proj_n(half_bank(2, b), (h_hi, h_lo), nodes(b), v0_hi, v0_lo)
                m.then_inc(S("v_done"), 1)

            def apply_rel(half):
                for b in (2 * half, 2 * half + 1):
                    cols = slice(b * D, (b + 1) * D)
                    for i, (r, v) in enumerate(((rel_hi, v_hi), (rel_hi, v_lo), (rel_lo, v_hi))):
                        m = pe.matmul(half_bank(2, b), r[:, nodes(b)], v[:, cols], start=(i == 0), stop=(i == 2),
                                      skip_group_check=True)
                return m

            l0(0, True)
            pe.wait_ge(S("nrm_ready"), 1)
            pe.wait_ge(su_dve, 3)
            pe.transpose(ps[:, 7, 0:N], adj_s[:], ident[:])
            for c in range(C):
                m = pe.matmul(ps[:, 7, D:2 * D], bv_rep[:, c, :], w_o[:, c, :], start=(c == 0), stop=(c == C - 1))
            m.then_inc(su_pe, 1)
            with pe.Fori(1, G) as g:
                l0(g, False)

            def project_qk(bank, w_hi, w_lo, name):
                for f in range(C):
                    cols = slice(f * P, (f + 1) * P)
                    for i, (w, h) in enumerate(((w_hi, h_hi), (w_lo, h_hi), (w_hi, h_lo))):
                        for c in range(C):
                            m = pe.matmul(ps[:, bank + f, :], w[:, c, cols], h[:, c, :], start=(i == 0 and c == 0),
                                          stop=(i == 2 and c == C - 1), skip_group_check=True)
                    m.then_inc(S(name), 1)

            def scores(g, half):
                if not half:
                    pe.wait_ge(S("q_ready"), C * g + C)
                    pe.wait_ge(S("k_ready"), C * g + 1)
                for b2 in range(PB):
                    for f in range(C):
                        for r in range(R):
                            if not half and b2 == 0 and f == 0 and r == 2 + C - 1:
                                pe.wait_ge(S("k_ready"), C * g + 2)
                            hd = slice(r * HD, (r + 1) * HD)
                            o = b2 * C * N + f * N
                            m = pe.matmul(ps[:, r, o:o + N], buf_a[hd, f, nodes(PB * half + b2)],
                                          buf_b[hd, f, nodes(PB * half + b2)], start=True, stop=True)
                m.then_inc(S("s_done"), 1)

            def attend(half, p, project):
                def turn_p(j):
                    b2, f = divmod(j, C)
                    pe.wait_ge(S("prob_ready"), 2 * p + b2 + 1)
                    if j >= 2:
                        pe.wait_ge(S("pt_ready"), 4 * p + j - 1)
                    for r in range(R):
                        m = pe.transpose(ps[:, 4 + f, nodes(r)], pr[:, half, b2, r, f, :], ident[:])
                    m.then_inc(S("pt_done"), 1)

                def apply_p(j):
                    b2, f = divmod(j, C)
                    pe.wait_ge(S("pt_ready"), 4 * p + j + 1)
                    if j == 0 and not (isinstance(p, int) and p == 0):
                        pe.wait_ge(S("o_lo_ready"), p)
                    o = f * PB * N + b2 * N
                    for r in range(R):
                        v_cols = slice(f * P + r * HD, f * P + (r + 1) * HD)
                        m = pe.matmul(ps[r * HD:(r + 1) * HD, 6, o:o + N], vals[:, 0, 2 * half + b2, v_cols],
                                      pr_t[:, j % 2, r, :], start=True, stop=True)
                    return m

                turn_p(0)
                turn_p(1)
                if project:
                    project_o(p - 1, 0)
                apply_p(0)
                turn_p(2)
                apply_p(1)
                turn_p(3)
                if project:
                    project_o(p - 1, 1)
                apply_p(2)
                apply_p(3).then_inc(S("pv_done"), 1)

            def project_o(p, b2):
                if b2 == 0:
                    pe.wait_ge(S("o_lo_ready"), p + 1)
                    if not (isinstance(p, int) and p == 0):
                        pe.wait_ge(S("fin1"), p)
                m = proj_n(half_bank(7, b2), (o_hi, o_lo), nodes(b2), o1_hi, o1_lo)
                if b2 == PB - 1:
                    m.then_inc(S("y_done"), 1)

            def v1():
                for b in range(GB):
                    m = proj_n(half_bank(4, b), (h_hi, h_lo), nodes(b), v1_hi, v1_lo)
                m.then_inc(S("v1_done"), 1)

            def l1(g, first):
                if not first:
                    pe.wait_ge(S("masked"), 4 * g)
                pe.wait_ge(hi_ready, g + G + 1)
                pe.wait_ge(lo_ready, g + G + 1)
                project_qk(0, q1_hi, q1_lo, "q_done")
                if first:
                    pe.wait_ge(S("fin0"), G)
                project_qk(2, k1_hi, k1_lo, "k_done")
                scores(g, 0)
                if not first:
                    attend(1, 2 * g - 1, True)
                if first:
                    v1()
                pe.wait_ge(S("masked"), 4 * g + 2)
                turn(g + G + 1, 0)
                if not first:
                    v1()
                pe.wait_ge(ht_ready, g + G + 2)
                scores(g, 1)
                pe.wait_ge(S("v1_ready"), g + 1)
                attend(0, 2 * g, not first)

            pe.wait_ge(su_lo, 1)
            l1(0, True)
            with pe.Fori(1, G) as g:
                l1(g, False)
            def sum_rows(g, first):
                pe.wait_ge(hi_ready, g + 2 * G + 1)
                if not first:
                    pe.wait_ge(S("e_ready"), g)
                for w in (s2_hi, s2_lo):
                    for c in range(C):
                        pe.matmul(ps[:, 4, :], w[:, c, :], h_hi[:, c, :], start=(w is s2_hi and c == 0), stop=False,
                                  skip_group_check=True)
                pe.wait_ge(lo_ready, g + 2 * G + 1)
                for c in range(C):
                    m = pe.matmul(ps[:, 4, :], s2_hi[:, c, :], h_lo[:, c, :], start=False, stop=(c == C - 1),
                                  skip_group_check=True)
                m.then_inc(S("s2_done"), 1)

            def project2(g, first, last):
                if not first:
                    pe.wait_ge(S("h_ready"), g)
                for b in (2, 3, 0, 1):
                    if b == 0 and not last:
                        turn(g + 2 * G + 1, 5)
                    if b == 0 and not (isinstance(g, int) and g < 2):
                        pe.wait_ge(S("ry_ready"), g - 1)
                    m = proj_n(ps[:, b, 0:D + 2], (h_hi, h_lo), nodes(b), w2_hi, w2_lo)
                m.then_inc(S("h_done"), 1)

            def turn_p2(g):
                pe.wait_ge(S("p2_ready"), g)
                for b in range(GB):
                    m = pe.transpose(ps[:, 7, nodes(b)], p2[:, b, :], ident[:])
                m.then_inc(S("p2_turned"), 1)

            def attend2(g, slot, last):
                pe.wait_ge(S("p2t_ready"), g)
                pe.wait_ge(S("h_ready"), g if last else g + 1)
                for b in range(GB):
                    m = pe.matmul(half_bank(0, b), p2_t[:, b, :], vals[:, slot, b, :], start=True, stop=True)
                m.then_inc(S("att_done"), 1)

            def l2(g, slot, first, last):
                sum_rows(g, first)
                project2(g, first, last)
                if not first:
                    turn_p2(g)
                    attend2(g, 1 - slot, False)

            pe.wait_ge(S("masked"), 2 * NP)
            pe.wait_ge(hi_ready, 2 * G + 1)
            pe.wait_ge(lo_ready, 2 * G + 1)
            project2(0, True, True)
            attend(1, NP - 1, True)
            sum_rows(0, True)
            for b2 in range(PB):
                project_o(NP - 1, b2)
            turn(2 * G + 1, 5)
            pe.wait_ge(S("fin1"), NP)
            l2(1, 0, False, False)
            with pe.Fori(0, (G - 4) // 2) as i:
                l2(2 * i + 2, 1, False, False)
                l2(2 * i + 3, 0, False, False)
            l2(G - 2, 1, False, False)
            l2(G - 1, 0, False, True)

            def gather(g, slot):
                pe.wait_ge(S("hn_ready"), g + 1)
                if not (isinstance(g, int) and g < 2):
                    pe.wait_ge(S("a_lo_ready"), g - 1)
                for b in range(GB):
                    for c in range(C):
                        m = pe.matmul(ps[:, A_BANK[slot] + c, nodes(b)], hn[slot][:, b, c * P:(c + 1) * P],
                                      norm_adj_t[:], start=True, stop=True)
                m.then_inc(S("a_done"), 1)

            def project3(g, slot, last=False):
                pe.wait_ge(S("a_lo_ready"), g + 1)
                if not (isinstance(g, int) and g == 0):
                    pe.wait_ge(S("fin3"), g)
                for b in range(GB):
                    m = proj_n(half_bank(0, b), (a_hi[:, slot], a_lo[slot]), nodes(b), w3_hi, w3_lo)
                    if b == GB - 1 or last and b == PB - 1:
                        m.then_inc(S("out3_done"), 1)

            gather(0, 0)
            pe.wait_ge(S("h_ready"), G)
            gather(1, 1)
            turn_p2(G)
            attend2(G, 0, True)
            pe.wait_ge(S("ry_ready"), G)
            project3(0, 0)
            with pe.Fori(0, (G - 2) // 2) as i:
                for k in range(2):
                    gather(2 * i + k + 2, k)
                    project3(2 * i + k + 1, 1 - k)
            project3(G - 1, 1, True)

        @block.vector
        def _(dve):
            def stats(n, g, ready, count):
                dve.wait_ge(ready, count)
                for b in range(GB):
                    i = dve.bn_stats(st[:, b, :], xg(g, b, 1))
                i.then_inc(bn_done, 1)
                if not (isinstance(n, int) and n == 0):
                    dve.wait_ge(nmr_ready, n)
                dve.wait_ge(bn_done, n + 1)
                dve.tensor_copy(st_seen[:], st[:, 0, 0:1])
                for b in range(GB):
                    i = dve.bn_aggr(mv[:, b, :], st[:, b, :])
                i.then_inc(S("mv_own"), 1)
                dve.wait_ge(S("mv_own"), n + 1)
                dve.tensor_scalar(neg_mean[:], mv[:, :, 0], -1.0, None, ALU.mult).then_inc(stat_ready, 1)

            def hi_part(n):
                dve.wait_ge(ht_ready, n + 1)
                dve.tensor_copy(h_hi[:], h_t[:]).then_inc(hi_ready, 1)

            def lo_part(n):
                dve.wait_ge(hi_ready, n + 1)
                dve.tensor_tensor(h_lo[:], h_t[:], f32(h_hi[:]), ALU.subtract).then_inc(lo_ready, 1)

            own = [0]

            def mine(i):
                own[0] += 1
                i.then_inc(S("su_own"), 1)
                dve.wait_ge(S("su_own"), own[0])

            def split(hi, lo, src):
                mine(dve.tensor_copy(hi, src))
                return dve.tensor_tensor(lo, src, f32(hi), ALU.subtract)

            stats(0, 0, x_in, 16)
            dve.wait_ge(w_in, 16 * len(loads))
            dve.tensor_reduce(deg[:], adj_n[:], AX_X, ALU.add).then_inc(S("deg_ready"), 1)
            dve.wait_ge(su_pe, 1)
            split(m_hi[:], m_lo[:], ps[:, 0:2, 0:D]).then_inc(su_dve, 1)
            hi_part(0)
            lo_part(0)
            split(v0_hi[:], v0_lo[:], ps[:, 2:4, 0:D]).then_inc(su_dve, 1)
            stats(1, 1, x_in, 32)
            dve.wait_ge(w_in2, 16 * len(loads2))
            dve.wait_ge(su_pool, 1)
            dve.tensor_scalar(maskb[:], adj_n[:], -1.0, BIG, ALU.add, ALU.mult)
            dve.tensor_scalar(beta_i[:], ident[:], beta_c[:, 0:1], None, ALU.mult)
            mine(dve.tensor_scalar(b3_row[:], b3_row[:], -1.0, None, ALU.add))
            dve.tensor_scalar(bqs_c[:], bq_c[:], float(HD) ** -0.5, None, ALU.mult)
            for c in range(C):
                dve.tensor_scalar(bv_rep[:, c, :], ones[:], bv_c[:, c:c + 1], None, ALU.mult)
            dve.wait_ge(S("dis_ready"), 1)
            mine(dve.tensor_scalar(deg_pos[:], deg[:], 0.0, None, ALU.is_gt))
            mine(dve.tensor_tensor(dis[:], deg_pow[:], deg_pos[:], ALU.mult))
            dve.tensor_scalar(adj_s[:], adj_n[:], dis[:, 0:1], None, ALU.mult).then_inc(su_dve, 1)

            def setup_adj():
                dve.wait_ge(su_pe, 2)
                dve.tensor_scalar(norm_adj_t[:], ps[:, 7, 0:N], dis[:, 0:1], None, ALU.mult)
                dve.tensor_tensor(bo_row[:], ps[:, 7, D:2 * D], bo_row[:], ALU.add).then_inc(su_dve, 1)

            def v_lo_part(g, half):
                cols = slice(2 * half * D, 2 * (half + 1) * D)
                dve.wait_ge(S("v_hi_ready"), 2 * g + half + 1)
                dve.tensor_tensor(v_lo[:, cols], ps[:, 2 + half, :], f32(v_hi[:, cols]), ALU.subtract)\
                   .then_inc(S("v_lo_ready"), 1)

            def l0(g, stats_args, between=None):
                if stats_args:
                    stats(g + 2, *stats_args)
                v_lo_part(g, 0)
                dve.wait_ge(S("rel_done"), g + 1)
                dve.tensor_tensor(rel[:].rearrange("p (b n) -> p b n", b=GB),
                                  ps[:, 4, :].rearrange("p (b n) -> p b n", b=GB),
                                  bc(adj_n[:], GB), ALU.mult).then_inc(S("rel_ready"), 1)
                dve.wait_ge(S("rel_hi_ready"), g + 1)
                dve.tensor_tensor(rel_lo, rel[:], f32(rel_hi), ALU.subtract).then_inc(S("rel_lo_ready"), 1)
                v_lo_part(g, 1)
                hi_part(g + 1)
                dve.wait_ge(S("nrm_done"), g + 1)
                dve.tensor_copy(nrm[:], ps[:, 7, 0:GB]).then_inc(S("nrm_ready"), 1)
                lo_part(g + 1)
                if between:
                    between()
                dve.wait_ge(S("out0_done"), g + 1)
                dve.wait_ge(S("rnrm_ready"), g + 1)
                for b in range(GB):
                    i = dve.scalar_tensor_tensor(xg(g, b, 1), ps[:, 2 + b // 2, (b % 2) * D:(b % 2 + 1) * D],
                                                 rnrm[:, b:b + 1], xg(g, b, 1), ALU.mult, ALU.add)
                i.then_inc(S("fin0"), 1)

            l0(0, (2, x_in, 48), setup_adj)
            with dve.Fori(1, G - 2) as g:
                l0(g, (g + 2, x_in, g * 16 + 48))
            l0(G - 2, (0, S("fin0"), 1))
            l0(G - 1, (1, S("fin0"), 2))

            for c in range(C):
                for t in range(2):
                    mine(dve.tensor_tensor(w2junk[:], w2x[:, c, 0:D], a_row[:, t, :], ALU.mult))
                    mine(dve.tensor_reduce(w2c[:, c, t:t + 1], w2junk[:], AX_X, ALU.add))
            for c in range(C):
                dve.tensor_copy(w2x[:, c, D:D + 2], w2c[:, c, 0:1].broadcast_to([P, 2]))
                mine(dve.tensor_scalar(w2rep[:, c, :], ones[:], w2c[:, c, 1:2], None, ALU.mult))
            split(w2_hi[:], w2_lo[:], w2x[:])
            split(s2_hi[:], s2_lo[:], w2rep[:])

            def mask_max(g, half):
                p = 2 * g + half
                dve.wait_ge(S("s_done"), p + 1)
                for b2 in range(PB):
                    if not (isinstance(g, int) and p < 1):
                        dve.wait_ge(S("shifted"), 2 * p + b2 - 1)
                    dve.tensor_tensor(sc[:, b2], ps[:, 0:R, b2 * C * N:(b2 + 1) * C * N].rearrange(
                        "p r (f n) -> p r f n", f=C),
                        maskb[:].unsqueeze(1).unsqueeze(1).broadcast_to([P, R, C, N]), ALU.add)\
                       .then_inc(S("masked"), 1)
                    dve.wait_ge(S("masked"), 2 * p + b2 + 1)
                    dve.tensor_reduce(mx[:, b2, :], sc[:, b2].rearrange("p r f n -> p (r f) n"), AX_X,
                                      ALU.max).then_inc(S("max_ready"), 1)

            def sum_probs(p, half, b2):
                dve.wait_ge(S("exp_ready"), 2 * p + b2 + 1)
                dve.tensor_reduce(sums[:, b2], pr[:, half, b2].rearrange("p r f n -> p (r f) n"), AX_X, ALU.add)\
                   .then_inc(S("sums_own"), 1)
                dve.wait_ge(S("sums_own"), 2 * p + b2 + 1)
                if not (isinstance(p, int) and p == 0):
                    dve.wait_ge(S("prob_ready"), 2 * p + b2 - 1)
                dve.reciprocal(rinv[:, b2], sums[:, b2]).then_inc(S("rinv_ready"), 1)

            def o_lo_part(p):
                dve.wait_ge(S("o_hi_ready"), p + 1)
                dve.tensor_tensor(flat(o_lo[:]), ps[:, 6, :], f32(flat(o_hi[:])), ALU.subtract)\
                   .then_inc(S("o_lo_ready"), 1)

            def add1(g, half, p):
                dve.wait_ge(S("y_done"), p + 1)
                dve.wait_ge(S("bias1"), g + 1)
                dve.tensor_tensor(xg(g, PB * half, PB), ps[:, 7, :], xg(g, PB * half, PB), ALU.add)\
                   .then_inc(S("fin1"), 1)

            def l1(g, first, stats_args):
                mask_max(g, 0)
                if not first:
                    add1(g - 1, 0, 2 * g - 2)
                sum_probs(2 * g, 0, 0)
                if not first:
                    o_lo_part(2 * g - 1)
                sum_probs(2 * g, 0, 1)
                stats(g + G + 2, *stats_args)
                mask_max(g, 1)
                if not first:
                    add1(g - 1, 1, 2 * g - 1)
                sum_probs(2 * g + 1, 1, 0)
                o_lo_part(2 * g)
                sum_probs(2 * g + 1, 1, 1)

            l1(0, True, (2, S("fin0"), G))
            with dve.Fori(1, G - 2) as g:
                l1(g, False, (g + 2, S("fin0"), G))
            l1(G - 2, False, (0, S("fin1"), 2))
            l1(G - 1, False, (1, S("fin1"), 4))
            stats(2 * G + 2, 2, S("fin1"), 2 * 3)
            add1(G - 1, 0, NP - 2)
            o_lo_part(NP - 1)
            add1(G - 1, 1, NP - 1)

            def l2(g, slot, first, last, stats_args):
                dve.wait_ge(S("s2_done"), g + 1)
                dve.wait_ge(S("s1_ready"), g + 1)
                if not first:
                    dve.wait_ge(S("shifted2"), g)
                dve.tensor_tensor(e2[:], ps[:, 4, :].rearrange("p (b n) -> p b n", b=GB), bcol(s1[:], N),
                                  ALU.add).then_inc(S("e_ready"), 1)
                if not first:
                    p2t_part(g)
                dve.wait_ge(S("e_ready"), g + 1)
                dve.scalar_tensor_tensor(e2[:], e2[:], ALPHA, e2[:], ALU.mult, ALU.max).then_inc(S("lr_ready"), 1)
                if not last:
                    dve.wait_ge(hi_ready, g + 2 * G + 2)
                    dve.scalar_tensor_tensor(flat(h_lo[:]), flat(ps[:, 5:7, :]), 0.0, f32(flat(h_hi[:])), ALU.max,
                                             ALU.subtract).then_inc(lo_ready, 1)
                dve.wait_ge(S("masked2"), g + 1)
                dve.tensor_reduce(mx2[:], e2[:], AX_X, ALU.max).then_inc(S("max2_ready"), 1)
                stats(g + 2 * G + 3, *stats_args)
                dve.wait_ge(S("exp2_ready"), g + 1)
                dve.tensor_reduce(sum2[:], p2[:], AX_X, ALU.add).then_inc(S("sum2_own"), 1)
                dve.wait_ge(S("sum2_own"), g + 1)
                dve.reciprocal(ri2[:], sum2[:]).then_inc(S("ri2_ready"), 1)
                if not first:
                    elu_part(g, slot)

            def p2t_part(g):
                dve.wait_ge(S("p2_turned"), g)
                dve.tensor_tensor(p2_t[:], ps[:, 7, :].rearrange("p (b n) -> p b n", b=GB), bc(beta_i[:], GB),
                                  ALU.add).then_inc(S("p2t_ready"), 1)

            def elu_part(g, slot):
                dve.wait_ge(S("ry_ready"), g)
                if not (isinstance(g, int) and g < 3):
                    dve.wait_ge(S("fin2"), g - 2)
                dve.scalar_tensor_tensor(elu1[slot], flat(buf_b[:]), 1.0, flat(buf_a[:]), ALU.min, ALU.add)\
                   .then_inc(S("elu_ready"), 1)

            l2(0, 0, True, False, (3, S("fin1"), NP))
            l2(1, 1, False, False, (4, S("fin1"), NP))
            with dve.Fori(0, (G - 6) // 2) as i:
                for k in range(2):
                    l2(2 * i + k + 2, k, False, False, (2 * i + k + 5, S("fin1"), NP))
            l2(G - 4, 0, False, False, (G - 1, S("fin1"), NP))
            l2(G - 3, 1, False, False, (0, S("fin2"), 1))
            l2(G - 2, 0, False, False, (1, S("fin2"), 2))
            l2(G - 1, 1, False, True, (2, S("fin2"), 3))

            def lo3(g, slot):
                dve.wait_ge(S("a_hi_ready"), g + 1)
                dve.tensor_tensor(a_lo[slot][:], ps[:, A_BANK[slot]:A_BANK[slot] + C, :], f32(a_hi[:, slot]),
                                  ALU.subtract).then_inc(S("a_lo_ready"), 1)

            def add3(g):
                dve.wait_ge(S("out3_done"), g + 1)
                dve.wait_ge(S("bias3"), g + 1)
                dve.tensor_tensor(xg(g), flat(ps[:, 0:2, :]), xg(g), ALU.add).then_inc(S("fin3"), 1)

            def l3(g, slot, ahead):
                add3(g - 1)
                if ahead:
                    stats(g + 3 * G + 4, g + 4, S("fin2"), g + 5)
                lo3(g + 1, slot)

            lo3(0, 0)
            p2t_part(G)
            lo3(1, 1)
            stats(3 * G + 3, 3, S("fin2"), 4)
            elu_part(G, 0)
            stats(3 * G + 4, 4, S("fin2"), 5)
            with dve.Fori(0, (G - 6) // 2) as i:
                for k in range(2):
                    l3(2 * i + k + 1, k, True)
            for g in range(G - 5, G - 1):
                l3(g, (g + 1) % 2, g == G - 5)
            add3(G - 2)
            dve.wait_ge(S("bias3"), G)
            for i in range(2):
                dve.wait_ge(S("out3_done"), G + i)
                dve.tensor_tensor(xg(G - 1, PB * i, PB), ps[:, i, :], xg(G - 1, PB * i, PB), ALU.add)\
                   .then_inc(S("fin3"), 1)

        @block.scalar
        def _(act):
            def normalise(n, g):
                act.wait_ge(nmr_ready, n + 1)
                if not (isinstance(n, int) and n == 0):
                    act.wait_ge(turned, n)
                for b in range(GB):
                    i = act.activation(xn[:, b, :], xg(g, b, 1), ACT.Identity, bias=nmr[:, 0, b:b + 1],
                                       scale=rstd[:, 0, b:b + 1])
                i.then_inc(xn_ready, 1)

            def h_part(n, bank):
                act.wait_ge(turned, n + 1)
                act.activation(h_t[:], ps[:, bank:bank + 2, :], ACT.Relu).then_inc(ht_ready, 1)

            def hi_part(n):
                act.wait_ge(ht_ready, n + 1)
                act.activation(h_hi[:], h_t[:], ACT.Copy).then_inc(hi_ready, 1)

            normalise(0, 0)
            h_part(0, 5)

            def v_hi_part(g, half):
                act.wait_ge(S("v_done"), 2 * g + half + 1)
                act.activation(v_hi[:, 2 * half * D:2 * (half + 1) * D], ps[:, 2 + half, :], ACT.Copy)\
                   .then_inc(S("v_hi_ready"), 1)

            def l0(g, nxt):
                first = isinstance(g, int) and g == 0
                if not first:
                    normalise(g + 1, nxt)
                act.wait_ge(S("g_done"), g + 1)
                act.activation(buf_a[:], ps[:, 0:2, :], ACT.Copy).then_inc(S("gt_ready"), 1)
                if first:
                    normalise(g + 1, nxt)
                v_hi_part(g, 0)
                act.wait_ge(S("rel_ready"), g + 1)
                act.activation(rel_hi, rel[:], ACT.Copy).then_inc(S("rel_hi_ready"), 1)
                v_hi_part(g, 1)
                act.activation(rel2[:], rel[:], ACT.Square).then_inc(S("rel2_ready"), 1)
                h_part(g + 1, 5)

            l0(0, 1)
            act.wait_ge(w_in2, 16 * len(loads2))
            for i, (hi, lo) in enumerate(staged):
                act.activation(flat(hi[:]), wstage[:, i], ACT.Copy)
            act.activation(o1_hi[:], w_o[:], ACT.Copy).then_inc(su_hi, 1)
            with act.Fori(1, G - 1) as g:
                l0(g, g + 1)
            l0(G - 1, 0)

            def take_turned(p, j):
                act.wait_ge(S("pt_done"), 4 * p + j + 1)
                act.activation(flat(pr_t[:, j % 2]), ps[:, 4 + j % C, :], ACT.Copy).then_inc(S("pt_ready"), 1)

            def exponent(p, half, b2):
                act.wait_ge(S("shifted"), 2 * p + b2 + 1)
                t = pr[:, half, b2].rearrange("p r f n -> p (r f n)")
                act.activation(t, t, ACT.Exp).then_inc(S("exp_ready"), 1)

            def o_hi_part(p):
                act.wait_ge(S("pv_done"), p + 1)
                if not (isinstance(p, int) and p == 0):
                    act.wait_ge(S("y_done"), p)
                act.activation(flat(o_hi[:]), ps[:, 6, :], ACT.Copy).then_inc(S("o_hi_ready"), 1)

            def take_q(g, f):
                act.wait_ge(S("q_done"), C * g + f + 1)
                act.activation(buf_a[:, f, :], ps[:, f, :], ACT.Identity, bias=bqs_c[:, f:f + 1],
                               scale=float(HD) ** -0.5).then_inc(S("q_ready"), 1)

            def l1(g, first, nxt):
                take_q(g, 1)
                for f in range(C):
                    act.wait_ge(S("k_done"), C * g + f + 1)
                    act.activation(buf_b[:, f, :], ps[:, 2 + f, :], ACT.Identity, bias=bk_c[:, f:f + 1])\
                       .then_inc(S("k_ready"), 1)
                normalise(g + G + 1, nxt)
                if not first:
                    for j in range(PB * C):
                        take_turned(2 * g - 1, j)
                if first:
                    h_part(g + G + 1, 0)
                exponent(2 * g, 0, 0)
                if not first:
                    o_hi_part(2 * g - 1)
                    h_part(g + G + 1, 0)
                exponent(2 * g, 0, 1)
                act.wait_ge(S("v1_done"), g + 1)
                act.activation(flat(vals[:, 0]), flat(ps[:, 4:6, :]), ACT.Copy).then_inc(S("v1_ready"), 1)
                hi_part(g + G + 1)
                for j in range(PB * C):
                    take_turned(2 * g, j)
                exponent(2 * g + 1, 1, 0)
                o_hi_part(2 * g)
                if not (isinstance(g, int) and g == G - 1):
                    take_q(g + 1, 0)
                exponent(2 * g + 1, 1, 1)

            act.wait_ge(su_dve, 3)
            take_q(0, 0)
            l1(0, True, 1)
            with act.Fori(1, G - 1) as g:
                l1(g, False, g + 1)
            l1(G - 1, False, 0)
            def natural(g, slot):
                act.wait_ge(nmr_ready, g + 3 * G + 1)
                if not (isinstance(g, int) and g < 2):
                    act.wait_ge(S("a_done"), g - 1)
                for b in range(GB):
                    i = act.activation(hn[slot][:, b, :], xg(g, b, 1), ACT.Relu, bias=nmr[:, slot, b:b + 1],
                                       scale=rstd[:, slot, b:b + 1])
                i.then_inc(S("hn_ready"), 1)

            def output2(g, first):
                act.wait_ge(S("att_done"), g)
                if not first:
                    act.wait_ge(S("elu_ready"), g - 1)
                act.activation(buf_b[:], ps[:, 0:2, :], ACT.Exp).then_inc(S("ey_done"), 1)
                act.activation(buf_a[:], ps[:, 0:2, :], ACT.Relu).then_inc(S("ry_ready"), 1)

            def take_h(g, slot, first):
                act.wait_ge(S("h_done"), g + 1)
                if not first:
                    act.wait_ge(S("e_ready"), g)
                act.activation(s1[:], ps[:, 0:GB, D], ACT.Copy).then_inc(S("s1_ready"), 1)
                act.activation(vals[:, slot], ps[:, 0:GB, 0:D], ACT.Copy).then_inc(S("h_ready"), 1)

            def l2(g, slot, last, nxt):
                if not (isinstance(g, int) and g == 0):
                    take_h(g, slot, False)
                if not last:
                    act.wait_ge(turned, g + 2 * G + 2)
                    act.activation(h_hi[:], ps[:, 5:7, :], ACT.Relu).then_inc(hi_ready, 1)
                if nxt is not None:
                    normalise(g + 2 * G + 2, nxt)
                if last:
                    natural(1, 1)
                if not (isinstance(g, int) and g == 0):
                    output2(g, isinstance(g, int) and g == 1)
                act.wait_ge(S("shifted2"), g + 1)
                act.activation(p2[:], p2[:], ACT.Exp).then_inc(S("exp2_ready"), 1)

            normalise(2 * G + 1, 1)
            take_h(0, 1, True)
            for j in range(PB * C):
                take_turned(NP - 1, j)
            o_hi_part(NP - 1)
            l2(0, 1, False, 2)
            l2(1, 0, False, 3)
            with act.Fori(0, (G - 4) // 2) as i:
                l2(2 * i + 2, 1, False, 2 * i + 4)
                l2(2 * i + 3, 0, False, 2 * i + 5)
            l2(G - 2, 1, False, None)
            natural(0, 0)
            l2(G - 1, 0, True, None)

            def hi3(g, slot):
                act.wait_ge(S("a_done"), g + 1)
                act.activation(a_hi[:, slot], ps[:, A_BANK[slot]:A_BANK[slot] + C, :], ACT.Copy)\
                   .then_inc(S("a_hi_ready"), 1)

            hi3(0, 0)
            hi3(1, 1)
            output2(G, False)
            natural(2, 0)
            with act.Fori(0, (G - 4) // 2) as i:
                for k in range(2):
                    natural(2 * i + k + 3, 1 - k)
                    hi3(2 * i + k + 2, k)
            natural(G - 1, 1)
            hi3(G - 2, 0)
            hi3(G - 1, 1)

        @block.gpsimd
        def _(pool):
            def rstd_part(n, last_used, count, slot=0):
                pool.wait_ge(stat_ready, n + 1)
                pool.tensor_tensor(veps[:], mv[:, :, 1], eps_c[:], ALU.add).then_inc(veps_done, 1)
                if last_used is not None:
                    pool.wait_ge(last_used, count)
                pool.wait_ge(veps_done, n + 1)
                pool.tensor_tensor(rstd[:, slot], veps[:], expo[:], ALU.pow).then_inc(rstd_done, 1)
                pool.wait_ge(rstd_done, n + 1)
                pool.tensor_tensor(nmr[:, slot], neg_mean[:], rstd[:, slot], ALU.mult).then_inc(nmr_ready, 1)

            def lo_part(n):
                pool.wait_ge(hi_ready, n + 1)
                pool.tensor_tensor(h_lo[:], h_t[:], f32(h_hi[:]), ALU.subtract).then_inc(lo_ready, 1)

            def add_row(g, row, name):
                v = xg(g).rearrange("p (b d) -> p b d", b=GB)
                pool.tensor_tensor(v, v, row[:].unsqueeze(1).broadcast_to([P, GB, D]), ALU.add).then_inc(S(name), 1)

            pool.memset(expo[:], -0.5)
            pool.memset(eps_c[:], EPS)
            pool.memset(ones[:], 1.0)
            pool.memset(ident[:], 0.0).then_inc(S("su_zero"), 1)
            pool.wait_ge(S("su_zero"), 1)
            pool.affine_select(out=ident[:], in_=ident[:], compare_op=ALU.not_equal, fill=1.0, base=0,
                               pattern=[[-1, P]], channel_multiplier=1).then_inc(su_pool, 1)
            pool.wait_ge(su_pool, 1)
            rstd_part(0, None, 0)
            pool.wait_ge(S("deg_ready"), 1)
            pool.tensor_scalar(deg_safe[:], deg[:], TINY, None, ALU.max).then_inc(S("dis_own"), 1)
            rstd_part(1, xn_ready, 1)
            pool.wait_ge(S("dis_own"), 1)
            pool.tensor_tensor(deg_pow[:], deg_safe[:], expo[:, 0:1], ALU.pow).then_inc(S("dis_ready"), 1)

            def l0(g):
                rstd_part(g + 2, xn_ready, g + 2)
                pool.wait_ge(S("nrm_ready"), g + 1)
                pool.tensor_tensor(rnrm[:], nrm[:], expo[:], ALU.pow).then_inc(S("rnrm_ready"), 1)

            l0(0)
            pool.wait_ge(su_hi, 1)
            for i, (hi, lo) in enumerate(staged):
                pool.tensor_tensor(flat(lo[:]), wstage[:, i], f32(flat(hi[:])), ALU.subtract)
            pool.tensor_tensor(o1_lo[:], w_o[:], f32(o1_hi[:]), ALU.subtract).then_inc(su_lo, 1)
            with pool.Fori(1, G) as g:
                l0(g)

            def shift_scores(g, half, b2):
                p = 2 * g + half
                pool.wait_ge(S("max_ready"), 2 * p + b2 + 1)
                if not (isinstance(g, int) and p < 2):
                    pool.wait_ge(S("pt_done"), 4 * p - 4)
                pool.tensor_tensor(pr[:, half, b2].rearrange("p r f n -> p (r f) n"),
                                   sc[:, b2].rearrange("p r f n -> p (r f) n"), bcol(mx[:, b2, :], N),
                                   ALU.subtract).then_inc(S("shifted"), 1)

            def scale_probs(p, half, b2):
                pool.wait_ge(S("rinv_ready"), 2 * p + b2 + 1)
                t = pr[:, half, b2].rearrange("p r f n -> p (r f) n")
                pool.tensor_tensor(t, t, bcol(rinv[:, b2, :], N), ALU.mult).then_inc(S("prob_ready"), 1)

            def l1(g):
                for half in range(2):
                    for b2 in range(PB):
                        shift_scores(g, half, b2)
                    if half:
                        rstd_part(g + G + 2, xn_ready, g + G + 2)
                    for b2 in range(PB):
                        scale_probs(2 * g + half, half, b2)
                    if not half:
                        lo_part(g + G + 1)
                pool.wait_ge(S("fin0"), g + 1)
                add_row(g, bo_row, "bias1")

            pool.wait_ge(su_dve, 4)
            l1(0)
            with pool.Fori(1, G) as g:
                l1(g)

            def add2(g, slot):
                pool.wait_ge(S("elu_ready"), g)
                pool.tensor_tensor(xg(g - 1), elu1[slot], xg(g - 1), ALU.add).then_inc(S("fin2"), 1)

            def scale2(g):
                pool.wait_ge(S("ri2_ready"), g + 1)
                pool.tensor_tensor(p2[:], p2[:], bcol(ri2[:], N), ALU.mult).then_inc(S("p2_ready"), 1)

            def l2(g, slot):
                pool.wait_ge(S("lr_ready"), g + 1)
                pool.tensor_tensor(e2[:], e2[:], bc(adj_n[:], GB), ALU.mult).then_inc(S("masked2"), 1)
                pool.wait_ge(S("max2_ready"), g + 1)
                if not (isinstance(g, int) and g == 0):
                    pool.wait_ge(S("p2_turned"), g)
                pool.tensor_tensor(p2[:], e2[:], bcol(mx2[:], N), ALU.subtract).then_inc(S("shifted2"), 1)
                if not (isinstance(g, int) and g < 2):
                    add2(g - 1, 1 - slot)
                scale2(g)
                if not (isinstance(g, int) and g > G - 3):
                    rstd_part(g + 2 * G + 3, xn_ready, g + 2 * G + 3)

            rstd_part(2 * G + 2, xn_ready, 2 * G + 2)
            l2(0, 0)
            l2(1, 1)
            with pool.Fori(0, (G - 4) // 2) as i:
                for k in range(2):
                    l2(2 * i + k + 2, k)
            l2(G - 2, 0)
            rstd_part(3 * G + 1, None, 0, 1)
            l2(G - 1, 1)
            rstd_part(3 * G + 2, S("hn_ready"), 1, 0)
            add2(G - 1, 1)

            add_row(0, b3_row, "bias3")
            rstd_part(3 * G + 3, S("hn_ready"), 2, 1)
            add2(G, 0)
            add_row(1, b3_row, "bias3")
            with pool.Fori(0, (G - 4) // 2) as i:
                for k in range(2):
                    rstd_part(2 * i + k + 3 * G + 4, S("hn_ready"), 2 * i + k + 3, k)
                    add_row(2 * i + k + 2, b3_row, "bias3")
            pool.wait_ge(S("hn_ready"), G)
            add_row(G - 2, b3_row, "bias3")
            add_row(G - 1, b3_row, "bias3")


_INS = ['x', 'adj', 'L0_gnn_Wq', 'L0_gnn_Wk', 'L0_gnn_Wv', 'L1_gnn_Wq', 'L1_gnn_bq', 'L1_gnn_Wk', 'L1_gnn_bk',
        'L1_gnn_Wv', 'L1_gnn_bv', 'L1_gnn_Wo', 'L1_gnn_bo', 'L2_gnn_W', 'L2_gnn_a', 'L2_gnn_beta',
        'L3_gnn_weight', 'L3_gnn_bias']
_OUTS = [((64, 128, 256), 'float32')]


def kernel(**inputs):
    import numpy as _np
    import concourse.bacc as _bacc
    from concourse import mybir as _mybir
    from concourse.bass_utils import run_bass_kernel_spmd as _run

    nc = _bacc.Bacc("TRN2", target_bir_lowering=False, num_devices=1)
    arrays, args = {}, []
    for name in _INS:
        a = _np.ascontiguousarray(inputs[name])
        arrays[f"in_{name}_dram"] = a
        args.append(nc.dram_tensor(f"in_{name}_dram", a.shape, _mybir.dt.from_np(a.dtype), kind="ExternalInput").ap())
    for i, (shape, dtype) in enumerate(_OUTS):
        dt = _mybir.dt.from_np(_np.dtype(dtype))
        args.append(nc.dram_tensor(f"out_{i}_dram", shape, dt, kind="ExternalOutput").ap())
    four_layer_graph_kernel(nc, *args)
    r = _run(nc, [arrays], core_ids=[0])
    got = tuple(r.results[0][f"out_{i}_dram"] for i in range(len(_OUTS)))
    return got[0]
```
